# Optimizing a Trainium2 kernel written in Bass

```python
import numpy as np
import jax
import jax.numpy as jnp

def _softmax(x, axis=-1):
    return jax.nn.softmax(x, axis=axis)

def _gelu(x):
    return jax.nn.gelu(x, approximate=True)

def _silu(x):
    return jax.nn.silu(x)

def _sigmoid(x):
    return jax.nn.sigmoid(x)

def _layernorm(x, axis=-1, eps=1e-05):
    m = jnp.mean(x, axis=axis, keepdims=True)
    v = jnp.var(x, axis=axis, keepdims=True)
    return (x - m) / jnp.sqrt(v + eps)

def _scatter_add(tgt, idx, src, axis=0):
    return tgt.at[idx].add(src)

def _segment_sum(src, seg, n):
    return jax.ops.segment_sum(src, seg, n)
kernel_name = 'mk_xattn_seq_d1_seqx_r2_b31990'

def setup_inputs(seed: int=0):
    np.random.seed(seed)
    _w = jnp.asarray

    def _rec_inputs():
        import jax
        import jax.numpy as jnp
        _rk = jax.random.key(seed)
        x = -0.0003929 + 0.9999 * jax.random.normal(jax.random.fold_in(_rk, 1), (4, 2048, 512), jnp.float32)
        _lenS = 2048 - jax.random.randint(jax.random.fold_in(_rk, 7), (4,), 0, max(1, 2048 // 4) + 1, jnp.int32)
        _lenS2 = 77 - jax.random.randint(jax.random.fold_in(_rk, 8), (4,), 0, max(1, 77 // 4) + 1, jnp.int32)
        _ctx_768P = jax.random.normal(jax.random.fold_in(_rk, 11), (4, 16, 384), jnp.float32)
        _ctx_768c = jax.random.dirichlet(jax.random.fold_in(_rk, 511), 0.3 * jnp.ones((16,), jnp.float32), (4, 77))
        _ctx_768t = jnp.einsum('bsk,bkd->bsd', _ctx_768c, _ctx_768P)
        _ctx_768t = _ctx_768t * jax.lax.rsqrt(jnp.mean(jnp.square(_ctx_768t)) + 1e-12) * 0.953939
        ctx_768 = -5.15168e-05 + 0.999825 * (_ctx_768t + 0.3 * jax.random.normal(jax.random.fold_in(_rk, 611), (4, 77, 384), jnp.float32))
        return (x, ctx_768)
    x, ctx_768 = _rec_inputs()

    def _L0_xattn_setup():
        import jax, jax.numpy as jnp
        import numpy as np
        D_TEXT, D_AUDIO, D_HID = (512, 384, 512)
        EPS = 1e-05

        def layer_norm(x, gamma, beta):
            mu = jnp.mean(x, axis=-1, keepdims=True)
            var = jnp.mean(jnp.square(x - mu), axis=-1, keepdims=True)
            return (x - mu) * jax.lax.rsqrt(var + EPS) * gamma + beta
        key = jax.random.key(seed)
        ks = jax.random.split(key, 8)
        B, L, S = (16, 512, 1024)

        def xavier(k, shape):
            bound = np.sqrt(6.0 / (shape[0] + shape[1]))
            return jax.random.uniform(k, shape, jnp.float32, -bound, bound)
        return {'H_l': jax.random.normal(ks[0], (B, L, D_TEXT), jnp.float32), 'H_a': jax.random.normal(ks[1], (B, S, D_AUDIO), jnp.float32), 'W_text': xavier(ks[2], (D_TEXT, D_HID)), 'b_text': jnp.zeros((D_HID,), jnp.float32), 'W_audio': xavier(ks[3], (D_AUDIO, D_HID)), 'b_audio': jnp.zeros((D_HID,), jnp.float32), 'W_out': xavier(ks[4], (D_HID, D_HID)), 'b_out': jnp.zeros((D_HID,), jnp.float32), 'g1': jnp.ones((D_HID,), jnp.float32), 'beta1': jnp.zeros((D_HID,), jnp.float32), 'g2': jnp.ones((D_HID,), jnp.float32), 'beta2': jnp.zeros((D_HID,), jnp.float32), 'g_out': jnp.ones((D_HID,), jnp.float32), 'beta_out': jnp.zeros((D_HID,), jnp.float32)}
    _L0_xattn_all = _L0_xattn_setup()
    _L0_xattn_in = {k: v for k, v in _L0_xattn_all.items() if k in ('W_text', 'b_text', 'W_audio', 'b_audio', 'W_out', 'b_out', 'g1', 'beta1', 'g2', 'beta2', 'g_out', 'beta_out')}
    del _L0_xattn_all
    return {'x': x, 'ctx_768': ctx_768, 'L0_xattn_W_text': _L0_xattn_in['W_text'], 'L0_xattn_b_text': _L0_xattn_in['b_text'], 'L0_xattn_W_audio': _L0_xattn_in['W_audio'], 'L0_xattn_b_audio': _L0_xattn_in['b_audio'], 'L0_xattn_W_out': _L0_xattn_in['W_out'], 'L0_xattn_b_out': _L0_xattn_in['b_out'], 'L0_xattn_g1': _L0_xattn_in['g1'], 'L0_xattn_beta1': _L0_xattn_in['beta1'], 'L0_xattn_g2': _L0_xattn_in['g2'], 'L0_xattn_beta2': _L0_xattn_in['beta2'], 'L0_xattn_g_out': _L0_xattn_in['g_out'], 'L0_xattn_beta_out': _L0_xattn_in['beta_out']}

def reference(x, ctx_768, L0_xattn_W_text, L0_xattn_b_text, L0_xattn_W_audio, L0_xattn_b_audio, L0_xattn_W_out, L0_xattn_b_out, L0_xattn_g1, L0_xattn_beta1, L0_xattn_g2, L0_xattn_beta2, L0_xattn_g_out, L0_xattn_beta_out):
    import jax
    import jax.numpy as jnp

    def _L0_xattn_ref(H_l, H_a, W_text, b_text, W_audio, b_audio, W_out, b_out, g1, beta1, g2, beta2, g_out, beta_out):
        import jax, jax.numpy as jnp
        import numpy as np
        D_TEXT, D_AUDIO, D_HID = (512, 384, 512)
        EPS = 1e-05

        def layer_norm(x, gamma, beta):
            mu = jnp.mean(x, axis=-1, keepdims=True)
            var = jnp.mean(jnp.square(x - mu), axis=-1, keepdims=True)
            return (x - mu) * jax.lax.rsqrt(var + EPS) * gamma + beta
        text_p = jnp.einsum('bld,dh->blh', H_l, W_text) + b_text
        audio_p = jnp.einsum('bsd,dh->bsh', H_a, W_audio) + b_audio
        Q = layer_norm(text_p, g1, beta1)
        K = layer_norm(audio_p, g2, beta2)
        V = audio_p
        scale = 1.0 / np.sqrt(D_HID).astype(np.float32)
        scores = jnp.einsum('blh,bsh->bls', Q, K) * scale
        alpha = jax.nn.softmax(scores, axis=-1)
        H_hyper = jnp.einsum('bls,bsh->blh', alpha, V)
        H_hyper = jnp.einsum('blh,hk->blk', H_hyper, W_out) + b_out
        return layer_norm(H_hyper + H_l, g_out, beta_out)
    x = _L0_xattn_ref(x, ctx_768, L0_xattn_W_text, L0_xattn_b_text, L0_xattn_W_audio, L0_xattn_b_audio, L0_xattn_W_out, L0_xattn_b_out, L0_xattn_g1, L0_xattn_beta1, L0_xattn_g2, L0_xattn_beta2, L0_xattn_g_out, L0_xattn_beta_out)
    return x

_drawn_inputs = setup_inputs


def setup_inputs(seed=0):
    import zlib

    import numpy as np

    out = dict(_drawn_inputs(seed))
    spreads = {'L0_xattn_b_text': (0.0, 0.431),
     'L0_xattn_b_audio': (0.0, 0.1),
     'L0_xattn_b_out': (0.0, 0.1),
     'L0_xattn_g1': (1.0, 0.2),
     'L0_xattn_beta1': (0.0, 0.413),
     'L0_xattn_g2': (1.0, 0.2),
     'L0_xattn_beta2': (0.0, 0.8),
     'L0_xattn_g_out': (1.0, 0.2),
     'L0_xattn_beta_out': (0.0, 0.1)}
    factors = {}
    for name, (base, spread) in spreads.items():
        noise = np.random.default_rng([zlib.crc32(name.encode()), seed]).standard_normal(out[name].shape)
        drawn = base * np.exp(spread * noise) if base else spread * noise
        out[name] = jnp.asarray(drawn.astype(out[name].dtype))
    for name, factor in factors.items():
        out[name] = (out[name] * factor).astype(out[name].dtype)
    return out
```

```python
from contextlib import ExitStack

import concourse.bass as bass
from concourse import mybir

F32 = mybir.dt.float32
F32R = mybir.dt.float32r
ALU = mybir.AluOpType
ACT = mybir.ActivationFunctionType
AX_X = mybir.AxisListType.X

P = 128
EPS = 1e-5


def cross_attention(nc, x, ctx, w_text, b_text, w_audio, b_audio, w_out, b_out,
                    g1, beta1, g2, beta2, g_out, beta_out, out):
    B, L, D = x.shape
    _, S, DA = ctx.shape
    H = w_text.shape[1]
    KD, KA, KH = D // P, DA // P, H // P
    SCALE = float(H) ** -0.5
    assert D == H == 4 * P and DA % P == 0 and S < P

    T = 2
    ROWS = T * P
    STEPS = B * L // ROWS
    PER_BATCH = L // ROWS
    BS = B * S
    SW = S + 3
    LIN, NXBAR = S, S + 1
    YW = D - P
    WIDTH = [YW + SW] + [D - k * P + SW for k in range(1, KD)]
    OFFSET = [0, WIDTH[0] + P] + [WIDTH[0] + P + sum(WIDTH[1:k]) for k in range(2, KD)]
    DIAG0 = WIDTH[0]
    COLS = sum(WIDTH) + P
    SCORE_AT = [OFFSET[k] + WIDTH[k] - SW for k in range(KD)]

    with ExitStack() as stack:
        def sb(name, shape, dt=F32):
            return stack.enter_context(nc.sbuf_tensor(name, shape, dt))

        def sem(name):
            return stack.enter_context(nc.semaphore(name))

        psT = stack.enter_context(nc.psum_tensor("psT", [P, T, 512], F32))
        psA = stack.enter_context(nc.psum_tensor("psA", [P, T, 512], F32))
        psB = stack.enter_context(nc.psum_tensor("psB", [P, 512], F32))
        psE = stack.enter_context(nc.psum_tensor("psE", [P, 512], F32))
        psO = stack.enter_context(nc.psum_tensor("psO", [P, T, 512], F32))

        ident = sb("ident", [P, P])
        proj_hi = sb("proj_hi", [P, B, COLS], F32R)
        proj_lo = sb("proj_lo", [P, B, COLS], F32R)
        val_hi = sb("val_hi", [S, B, H], F32R)
        val_lo = sb("val_lo", [S, B, H], F32R)
        score_c = sb("score_c", [P, B, SW])
        score_d = sb("score_d", [P, B, S])
        gain = sb("gain", [P, H])
        shift = sb("shift", [P, H])
        neg_half = sb("neg_half", [P, T])
        eps_sum = sb("eps_sum", [P, T])
        xs = sb("xs", [P, B, T, D])
        x_hi = sb("x_hi", [P, 2, T, D], F32R)
        x_lo = sb("x_lo", [P, 2, T, D], F32R)
        sc = sb("sc", [P, B, T, SW])
        quad_a = sb("quad_a", [P, B, T])
        quad_b = sb("quad_b", [P, B, T])
        var = sb("var", [P, B, T])
        rstd = sb("rstd", [P, B, T])
        logits = sb("logits", [P, 2, T, S])
        neg_max = sb("neg_max", [P, B, T])
        prob = sb("prob", [P, 2, T, S])
        prob_sum = sb("prob_sum", [P, B, T])
        inv_sum = sb("inv_sum", [P, B, T])
        prob_hi = sb("prob_hi", [S, 2, T * P], F32R)
        prob_lo = sb("prob_lo", [S, 2, T * P], F32R)
        hid = sb("hid", [P, 2, T, H])
        sq_sum = sb("sq_sum", [P, B, T])
        var2 = sb("var2", [P, B, T])
        rstd2 = sb("rstd2", [P, B, T])
        shift2 = sb("shift2", [P, B, T])
        zs = sb("zs", [P, B, T, H])
        waste_dve = sb("waste_dve", [P, 4, H], mybir.dt.bfloat16)
        waste_act = sb("waste_act", [P, 2, H], mybir.dt.bfloat16)

        wt = sb("wt", [P, KD, H])
        wa = sb("wa", [P, KA, H])
        wo = sb("wo", [P, KH, H])
        cx = sb("cx", [S, B, DA])
        cxT = sb("cxT", [P, KA, BS])
        wtT = sb("wtT", [P, KH, D])
        wgT = sb("wgT", [P, KH, D])
        vec_rows = sb("vec_rows", [4 * KH, P])
        vec_cols = sb("vec_cols", [P, 4 * KH])
        g1s = sb("g1s", [P, KH])
        bt_rows = sb("bt_rows", [P, H])
        beta1_rows = sb("beta1_rows", [P, H])
        bo_rows = sb("bo_rows", [P, H])
        btT = sb("btT", [P, KH, P])
        beta1T = sb("beta1T", [P, KH, P])
        sums = sb("sums", [P, 16])
        lin = sb("lin", [P, KD])
        vT = sb("vT", [P, KH, BS])
        osums = sb("osums", [P, KH + 1])
        room = [zs[:].rearrange("p b t h -> p (b t h)"), hid[:].rearrange("p c t h -> p (c t h)")]
        used = [0, 0]

        def borrow(where, n):
            used[where] += n
            assert used[where] <= room[where].shape[1]
            return room[where][:, used[where] - n:used[where]]

        vbuf = borrow(0, B * H).rearrange("p (b h) -> p b h", b=B)[0:S]
        kSq = borrow(0, KH * BS).rearrange("p (k n) -> p k n", k=KH)
        neg_half_k = borrow(0, BS)
        kT = borrow(1, KH * BS).rearrange("p (k n) -> p k n", k=KH)
        kvar, krstd = borrow(1, BS), borrow(1, BS)
        mean_of = borrow(1, P)

        wt_loaded, wa_loaded, wo_loaded = sem("wt_loaded"), sem("wa_loaded"), sem("wo_loaded")
        ctx_loaded, vec_loaded = sem("ctx_loaded"), sem("vec_loaded")
        bt_loaded, beta1_loaded, bo_loaded = sem("bt_loaded"), sem("beta1_loaded"), sem("bo_loaded")
        gs_loaded = sem("gs_loaded")
        ident_ready, ones_ready = sem("ident_ready"), sem("ones_ready")
        cxT_psum, cxT_ready = sem("cxT_psum"), sem("cxT_ready")
        vec_psum, vec_ready = sem("vec_psum"), sem("vec_ready")
        g1s_ready = sem("g1s_ready")
        vT_psum, vT_ready = sem("vT_psum"), sem("vT_ready")
        wc_ready, wtT_psum, wtT_ready, wgT_ready = sem("wc_ready"), sem("wtT_psum"), sem("wtT_ready"), sem("wgT_ready")
        bc_ready, rowsT_psum, rowsT_ready = sem("bc_ready"), sem("rowsT_psum"), sem("rowsT_ready")
        g_psum, g_hi, g_lo = sem("g_psum"), sem("g_hi"), sem("g_lo")
        mean_psum, kc_ready, ksq_ready, kvar_psum = sem("mean_psum"), sem("kc_ready"), sem("ksq_ready"), sem("kvar_psum")
        kvar_ready, krstd_ready, kn_ready, kT_ready = sem("kvar_ready"), sem("krstd_ready"), sem("kn_ready"), sem("kT_ready")
        gain_ready = sem("gain_ready")
        osums_ready, wo_ready, bo_ready = sem("osums_ready"), sem("wo_ready"), sem("bo_ready")
        val_psum, val_ready, val_hi_ready, val_lo_ready = sem("val_psum"), sem("val_ready"), sem("val_hi_ready"), sem("val_lo_ready")
        m_psum, m_hi, m_lo, cd_psum, cd_ready = sem("m_psum"), sem("m_hi"), sem("m_lo"), sem("cd_psum"), sem("cd_ready")
        proj_ready0, extras_ready = sem("proj_ready0"), sem("extras_ready")
        dve_own, pool_own, act_own = sem("dve_own"), sem("pool_own"), sem("act_own")

        x_loaded = [[sem(f"x_loaded{b}{t}") for t in range(T)] for b in range(B)]
        out_stored = [sem(f"out_stored{b}") for b in range(B)]
        xT_psum, x_hi_ready, x_lo_ready = sem("xT_psum"), sem("x_hi_ready"), sem("x_lo_ready")
        proj_psum, sc_ready, quad_ready = sem("proj_psum"), sem("sc_ready"), sem("quad_ready")
        var_sum, var_ready, rstd_ready = sem("var_sum"), sem("var_ready"), sem("rstd_ready")
        logits_ready = sem("logits_ready")
        max_ready = sem("max_ready")
        prob_ready = sem("prob_ready")
        inv_ready, probT_psum = sem("inv_ready"), sem("probT_psum")
        prob_hi_ready, prob_lo_ready = sem("prob_hi_ready"), sem("prob_lo_ready")
        mix_psum, hid_ready, sq_ready = sem("mix_psum"), sem("hid_ready"), sem("sq_ready")
        var2_ready, rstd2_ready, shift2_ready = sem("var2_ready"), sem("rstd2_ready"), sem("shift2_ready")
        z_ready, zg_ready, out_ready = sem("z_ready"), sem("zg_ready"), sem("out_ready")

        f32 = lambda ap: ap.bitcast(F32)

        def pipeline(eng, body):
            for b in range(B):
                body(b, 0, lambda lag, b=b: b - lag >= 0)
            with eng.Fori(1, STEPS // B) as i:
                for b in range(B):
                    body(b, i, lambda lag: True)
            for b in range(B):
                body(b, STEPS // B, lambda lag, b=b: b - lag < 0)

        def wait_if_positive(eng, s, per, i, const):
            value = per * B * i + const
            if isinstance(i, int) and value <= 0:
                return
            eng.wait_ge(s, value)

        block = stack.enter_context(nc.Block())

        @block.sync
        def _(sp):
            sp.dma_start(wt[:], w_text.rearrange("(k p) h -> p k h", p=P)).then_inc(wt_loaded, 16)
            sp.dma_start(wa[:], w_audio.rearrange("(k p) h -> p k h", p=P)).then_inc(wa_loaded, 16)
            sp.dma_start(wo[:], w_out.rearrange("(k p) h -> p k h", p=P)).then_inc(wo_loaded, 16)
            for n, row in enumerate((bo_rows,)):
                sp.dma_start(row[:], b_out.rearrange("(a h) -> a h", a=1).to_broadcast([P, H])).then_inc(bo_loaded, 16)
            sp.dma_start(gain[:], g_out.rearrange("(a h) -> a h", a=1).to_broadcast([P, H])).then_inc(gs_loaded, 16)
            sp.dma_start(shift[:], beta_out.rearrange("(a h) -> a h", a=1).to_broadcast([P, H])).then_inc(gs_loaded, 16)

            def body(b, i, live):
                if live(0):
                    for t in range(T):
                        wait_if_positive(sp, hid_ready, T, i, T * (b - B) + t + 1)
                        src = x[b, bass.ds(i * ROWS, ROWS), :].rearrange("(p t) d -> p t d", t=T)[:, t, :]
                        sp.dma_start(xs[:, b, t, :], src).then_inc(x_loaded[b][t], 16)
                if live(5):
                    q, j = (b - 5) % B, i + (b - 5) // B
                    wait_if_positive(sp, out_ready, T, i, T * (b - 5) + T)
                    dst = out[q, bass.ds(j * ROWS, ROWS), :].rearrange("(p t) d -> p t d", t=T)
                    sp.dma_start(dst, zs[:, q, :, :]).then_inc(out_stored[q], 16)

            for b in range(B):
                body(b, 0, lambda lag, b=b: b - lag >= 0)
            for b in range(B):
                body(b, 1, lambda lag, b=b: B + b - lag >= 0)
            with sp.Fori(2, STEPS // B) as i:
                for b in range(B):
                    body(b, i, lambda lag: True)
            for k in range(2):
                for b in range(B):
                    body(b, STEPS // B + k, lambda lag, s=k * B + b: lag > 0 and s - lag < 0)
            for b in range(B):
                sp.wait_ge(out_stored[b], 16 * PER_BATCH)

        @block.gpsimd
        def _(pool):
            nc.gpsimd.memset(ident[:], 1.0).then_inc(pool_own, 1)
            nc.gpsimd.memset(mean_of, 1.0 / H).then_inc(ones_ready, 1)
            nc.gpsimd.memset(neg_half[:], -0.5).then_inc(pool_own, 1)
            nc.gpsimd.memset(eps_sum[:], H * EPS).then_inc(pool_own, 1)
            nc.gpsimd.memset(neg_half_k, -0.5).then_inc(pool_own, 1)
            pool.wait_ge(pool_own, 1)
            nc.gpsimd.affine_select(out=ident[:], in_=ident[:], compare_op=ALU.is_equal, fill=0.0, base=0,
                                    pattern=[[-1, P]], channel_multiplier=1).then_inc(ident_ready, 1)
            nc.gpsimd.memset(score_c[:, :, S:SW], 0.0).then_inc(extras_ready, 1)
            for buf in (proj_hi, proj_lo):
                for k in range(KD):
                    at = SCORE_AT[k]
                    nc.gpsimd.memset(f32(buf[:, :, at + S:at + SW]), 0.0).then_inc(pool_own, 1)
            pool.wait_ge(pool_own, 4 + 2 * KD)
            for k in range(KD):
                at = SCORE_AT[k] + NXBAR
                nc.gpsimd.memset(f32(proj_hi[:, :, at:at + 1]), -1.0 / D).then_inc(extras_ready, 1)
            pool.wait_ge(osums_ready, 1)
            nc.gpsimd.tensor_scalar(bo_rows[:], bo_rows[:], osums[:, KH:KH + 1], 0.0, ALU.add, ALU.add).then_inc(bo_ready, 1)
            pool.wait_ge(pool_own, 4 + 2 * KD)
            for k in range(KH):
                nc.gpsimd.tensor_scalar(wo[:, k, :], wo[:, k, :], osums[:, k:k + 1], 0.0, ALU.add, ALU.add).then_inc(wo_ready, 1)
            pool.wait_ge(kvar_ready, 1)
            nc.gpsimd.tensor_tensor(krstd, kvar, neg_half_k, ALU.pow).then_inc(krstd_ready, 1)
            pool.wait_ge(gs_loaded, 32)
            nc.gpsimd.tensor_scalar(gain[:], gain[:], float(H) ** 0.5, 0.0, ALU.mult, ALU.add).then_inc(gain_ready, 1)
            pool.wait_ge(gain_ready, 1)

            def body(b, i, live):
                if live(2):
                    q = (b - 2) % B
                    wait_if_positive(pool, var_ready, 1, i, b - 1)
                    nc.gpsimd.tensor_tensor(rstd[:, q, :], var[:, q, :], neg_half[:, 0:T], ALU.pow).then_inc(rstd_ready, 1)
                if live(4):
                    q = (b - 4) % B
                    for t in range(T):
                        wait_if_positive(pool, z_ready, T, i, T * (b - 4) + t + 1)
                        nc.gpsimd.tensor_tensor(zs[:, q, t, :], zs[:, q, t, :], gain[:], ALU.mult).then_inc(zg_ready, 1)
                if live(3):
                    q = (b - 3) % B
                    wait_if_positive(pool, sq_ready, T, i, T * (b - 3) + T)
                    nc.gpsimd.tensor_tensor(var2[:, q, :], sq_sum[:, q, :], eps_sum[:], ALU.add).then_inc(var2_ready, 1)
                    wait_if_positive(pool, var2_ready, 1, i, b - 2)
                    nc.gpsimd.tensor_tensor(rstd2[:, q, :], var2[:, q, :], neg_half[:, 0:T], ALU.pow).then_inc(rstd2_ready, 1)
                    wait_if_positive(pool, rstd2_ready, 1, i, b - 2)
                    nc.gpsimd.tensor_tensor(shift2[:, q, :], sc[:, q, :, NXBAR], rstd2[:, q, :], ALU.mult).then_inc(shift2_ready, 1)
                if live(4):
                    q = (b - 4) % B
                    for t in range(T):
                        wait_if_positive(pool, zg_ready, T, i, T * (b - 4) + t + 1)
                        nc.gpsimd.tensor_tensor(zs[:, q, t, :], zs[:, q, t, :], shift[:], ALU.add).then_inc(out_ready, 1)

            pipeline(pool, body)

        @block.scalar
        def _(act):
            act.dma_start(cx[:], ctx.rearrange("b s d -> s b d")).then_inc(ctx_loaded, 16)
            for n, v in enumerate((g1, g2, beta2, b_audio)):
                act.dma_start(vec_rows[n * KH:(n + 1) * KH, :], v.rearrange("(k p) -> k p", p=P)).then_inc(vec_loaded, 16)
            act.dma_start(bt_rows[:], b_text.rearrange("(a h) -> a h", a=1).to_broadcast([P, H])).then_inc(bt_loaded, 16)
            act.dma_start(beta1_rows[:], beta1.rearrange("(a h) -> a h", a=1).to_broadcast([P, H])).then_inc(beta1_loaded, 16)

            for k in range(KA):
                act.wait_ge(cxT_psum, k + 1)
                nc.scalar.activation(cxT[:, k, :], (psA[:, 0], psA[:, 1], psB)[k][:, 0:BS], ACT.Copy).then_inc(cxT_ready, 1)
            act.wait_ge(vec_ready, 1)
            for k in range(KH):
                act.wait_ge(vT_psum, k + 1)
                nc.scalar.activation(vT[:, k, :], (psT[:, 0], psT[:, 1], psO[:, 0], psO[:, 1])[k][:, 0:BS], ACT.Identity,
                                     bias=vec_cols[:, 3 * KH + k:3 * KH + k + 1]).then_inc(vT_ready, 1)
            act.wait_ge(wo_loaded, 16)
            act.wait_ge(bo_loaded, 16)
            for k in range(KH + 1):
                row = wo[:, k, :] if k < KH else bo_rows[:]
                if k >= 2:
                    act.wait_ge(act_own, k - 1)
                last = nc.scalar.activation(waste_act[:, k % 2, :], row, ACT.Copy, scale=-1.0 / H, accum_out=osums[:, k:k + 1])
                last.then_inc(act_own if k < KH else osums_ready, 1)
            act.wait_ge(g1s_ready, 1)
            for k in range(KH):
                act.wait_ge(wtT_ready, k + 1)
                nc.scalar.activation(wgT[:, k, :], wtT[:, k, :], ACT.Copy, scale=g1s[:, k:k + 1]).then_inc(wgT_ready, 1)
            act.wait_ge(rowsT_psum, 1)
            for k in range(KH):
                nc.scalar.activation(btT[:, k, :], psB[:, k * P:(k + 1) * P], ACT.Copy, scale=g1s[:, k:k + 1])
            act.wait_ge(rowsT_psum, 2)
            nc.scalar.activation(beta1T[:], psE[:], ACT.Copy, scale=SCALE).then_inc(rowsT_ready, 1)
            for k in range(KH):
                act.wait_ge(kc_ready, k + 1)
                nc.scalar.activation(kSq[:, k, :], kT[:, k, :], ACT.Square).then_inc(ksq_ready, 1)
            for k in range(KD):
                act.wait_ge(g_psum, k + 1)
                src = (psA[:, 0], psA[:, 1], psO[:, 0], psO[:, 1])[k]
                at = DIAG0 if k == 0 else OFFSET[k]
                last = nc.scalar.activation(proj_hi[:, 0, at:at + P], src[:, 0:P], ACT.Copy, scale=1.0 / H)
                if k < KD - 1:
                    n = D - (k + 1) * P
                    at = 0 if k == 0 else OFFSET[k] + P
                    last = nc.scalar.activation(proj_hi[:, 0, at:at + n], src[:, P:P + n], ACT.Copy, scale=2.0 / H)
                last.then_inc(g_hi, 1)
            for b in range(B):
                act.wait_ge(val_ready, b + 1)
                nc.scalar.activation(val_hi[:, b, :], vbuf[:, b, :], ACT.Copy).then_inc(val_hi_ready, 1)
            for k in range(KH):
                act.wait_ge(kn_ready, k + 1)
                nc.scalar.activation(kT[:, k, :], kT[:, k, :], ACT.Identity,
                                     bias=vec_cols[:, 2 * KH + k:2 * KH + k + 1]).then_inc(kT_ready, 1)
            for k in range(KD):
                act.wait_ge(m_psum, k + 1)
                src = (psA[:, 0], psA[:, 1], psO[:, 0], psO[:, 1])[k]
                nc.scalar.activation(proj_hi[:, :, SCORE_AT[k]:SCORE_AT[k] + S],
                                     src[:, 0:BS].rearrange("p (b s) -> p b s", b=B), ACT.Copy).then_inc(m_hi, 1)

            def hi_part(b, i, t):
                wait_if_positive(act, xT_psum, T, i, T * b + t + 1)
                wait_if_positive(act, proj_psum, T, i, T * (b - 2) + t + 1)
                nc.scalar.activation(x_hi[:, b % 2, t, :], psT[:, t, :], ACT.Copy).then_inc(x_hi_ready, 1)

            def square(b, i, t):
                q = (b - 3) % B
                wait_if_positive(act, hid_ready, T, i, T * (b - 3) + t + 1)
                wait_if_positive(act, sq_ready, T, i, T * (b - 4) + t + 1)
                nc.scalar.activation(waste_act[:, t, :], hid[:, (b - 3) % 2, t, :], ACT.Square,
                                     bias=sc[:, q, t, NXBAR:NXBAR + 1],
                                     accum_out=sq_sum[:, q, t:t + 1]).then_inc(sq_ready, 1)

            def body(b, i, live):
                if live(0):
                    hi_part(b, i, 0)
                if live(3):
                    square(b, i, 0)
                if live(2):
                    q = (b - 2) % B
                    wait_if_positive(act, max_ready, 1, i, b - 1)
                    wait_if_positive(act, probT_psum, 1, i, b - 3)
                    for t in range(T):
                        nc.scalar.activation(prob[:, b % 2, t, :], logits[:, b % 2, t, :], ACT.Exp,
                                             bias=neg_max[:, q, t:t + 1],
                                             accum_out=prob_sum[:, q, t:t + 1]).then_inc(prob_ready, 1)
                if live(3):
                    square(b, i, 1)
                if live(0):
                    hi_part(b, i, 1)
                if live(2):
                    wait_if_positive(act, probT_psum, 1, i, b - 1)
                    wait_if_positive(act, mix_psum, T, i, T * (b - 4) + T)
                    nc.scalar.activation(prob_hi[:, b % 2, :], psE[0:S, 0:T * P], ACT.Copy).then_inc(prob_hi_ready, 1)
                if live(3):
                    q = (b - 3) % B
                    wait_if_positive(act, shift2_ready, 1, i, b - 2)
                    stored = i + (b - 3) // B
                    if not isinstance(stored, int) or stored > 0:
                        act.wait_ge(out_stored[q], 16 * stored)
                    for t in range(T):
                        nc.scalar.activation(zs[:, q, t, :], hid[:, (b - 3) % 2, t, :], ACT.Identity,
                                             bias=shift2[:, q, t:t + 1], scale=rstd2[:, q, t:t + 1]).then_inc(z_ready, 1)

            pipeline(act, body)

        @block.vector
        def _(dve):
            own = [0]

            def link(ins):
                own[0] += 1
                ins.then_inc(dve_own, 1)
                dve.wait_ge(dve_own, own[0])

            dve.wait_ge(wt_loaded, 16)
            link(nc.vector.reduce_sum(sums[:, 0:KD], wt[:], axis=AX_X))
            link(nc.vector.tensor_scalar(sums[:, 0:KD], sums[:, 0:KD], -1.0 / H, None, ALU.mult))
            for k in range(KD):
                nc.vector.tensor_scalar(wt[:, k, :], wt[:, k, :], sums[:, k:k + 1], None, ALU.add).then_inc(wc_ready, 1)
            dve.wait_ge(vec_psum, 1)
            nc.vector.tensor_copy(vec_cols[:], psE[:, 0:4 * KH]).then_inc(vec_ready, 1)
            dve.wait_ge(vec_ready, 1)
            nc.vector.tensor_scalar(g1s[:], vec_cols[:, 0:KH], SCALE, None, ALU.mult).then_inc(g1s_ready, 1)
            dve.wait_ge(bt_loaded, 16)
            link(nc.vector.reduce_sum(sums[:, 4:5], bt_rows[:], axis=AX_X))
            link(nc.vector.tensor_scalar(sums[:, 4:5], sums[:, 4:5], -1.0 / H, None, ALU.mult))
            nc.vector.tensor_scalar(bt_rows[:], bt_rows[:], sums[:, 4:5], None, ALU.add).then_inc(bc_ready, 1)
            for k in range(KH):
                dve.wait_ge(wtT_psum, k + 1)
                src = (psA[:, 0], psA[:, 1], psO[:, 0], psO[:, 1])[k]
                if k >= 2:
                    dve.wait_ge(vT_ready, k + 1)
                nc.vector.tensor_copy(wtT[:, k, :], src).then_inc(wtT_ready, 1)
            dve.wait_ge(bc_ready, 1)
            dve.wait_ge(wc_ready, KD)
            nc.vector.tensor_tensor_reduce(out=waste_dve[:, 3, :], in0=bt_rows[:], in1=bt_rows[:], scale=1.0 / H, scalar=EPS,
                                           op0=ALU.mult, op1=ALU.add, accum_out=sums[:, 5:6]).then_inc(dve_own, 1)
            for k in range(KD):
                if k == KD - 1:
                    dve.wait_ge(dve_own, own[0] + 1)
                nc.vector.tensor_tensor_reduce(out=waste_dve[:, (k + 3) % 3 if k < 3 else 3, :], in0=wt[:, k, :], in1=bt_rows[:],
                                               scale=2.0 / H, scalar=0.0,
                                               op0=ALU.mult, op1=ALU.add, accum_out=lin[:, k:k + 1]).then_inc(dve_own, 1)
            own[0] += 1 + KD
            dve.wait_ge(dve_own, own[0])
            dve.wait_ge(extras_ready, 1 + KD)
            for b in range(B):
                nc.vector.tensor_copy(score_c[:, b, LIN:LIN + 1], sums[:, 5:6])
            for k in range(KD):
                at = SCORE_AT[k] + LIN
                for b in range(B):
                    last = nc.vector.tensor_copy(proj_hi[:, b, at:at + 1], lin[:, k:k + 1])
            link(last)
            for k in range(KD):
                at = SCORE_AT[k] + LIN
                for b in range(B):
                    last = nc.vector.tensor_tensor(proj_lo[:, b, at:at + 1], lin[:, k:k + 1],
                                                   f32(proj_hi[:, b, at:at + 1]), ALU.subtract)
            dve.wait_ge(mean_psum, 1)
            for k in range(KH):
                nc.vector.tensor_tensor(kT[:, k, :], vT[:, k, :], psT[:, 0, 0:BS], ALU.subtract).then_inc(kc_ready, 1)
            for k in range(KD):
                dve.wait_ge(g_hi, k + 1)
                src = (psA[:, 0], psA[:, 1], psO[:, 0], psO[:, 1])[k]
                at = DIAG0 if k == 0 else OFFSET[k]
                last = nc.vector.scalar_tensor_tensor(proj_lo[:, 0, at:at + P], src[:, 0:P], 1.0 / H,
                                                      f32(proj_hi[:, 0, at:at + P]), ALU.mult, ALU.subtract)
                if k < KD - 1:
                    n = D - (k + 1) * P
                    at = 0 if k == 0 else OFFSET[k] + P
                    last = nc.vector.scalar_tensor_tensor(proj_lo[:, 0, at:at + n], src[:, P:P + n], 2.0 / H,
                                                          f32(proj_hi[:, 0, at:at + n]), ALU.mult, ALU.subtract)
                last.then_inc(g_lo, 1)
            dve.wait_ge(kvar_psum, 1)
            nc.vector.tensor_scalar(kvar, psT[:, 1, 0:BS], EPS, None, ALU.add).then_inc(kvar_ready, 1)
            for b in range(B):
                dve.wait_ge(val_psum, b + 1)
                if b == 0:
                    dve.wait_ge(bo_ready, 1)
                src = (psB, psE)[b % 2]
                nc.vector.tensor_tensor(vbuf[:, b, :], src[0:S, :], bo_rows[0:S, :], ALU.add).then_inc(val_ready, 1)
                if b == 0:
                    dve.wait_ge(krstd_ready, 1)
                    dve.wait_ge(ksq_ready, KH)
                    for k in range(KH):
                        nc.vector.scalar_tensor_tensor(kT[:, k, :], kT[:, k, :], vec_cols[:, KH + k:KH + k + 1], krstd,
                                                       ALU.mult, ALU.mult).then_inc(kn_ready, 1)
            dve.wait_ge(g_hi, KD)
            dve.wait_ge(g_lo, KD)
            for buf in (proj_hi, proj_lo):
                for at, n in [(0, YW), (DIAG0, P)] + [(OFFSET[k], D - k * P) for k in range(1, KD)]:
                    for b in range(1, B):
                        last = nc.vector.tensor_copy(buf[:, b, at:at + n], f32(buf[:, 0, at:at + n]))
            for b in range(B):
                dve.wait_ge(val_hi_ready, b + 1)
                nc.vector.tensor_tensor(val_lo[:, b, :], vbuf[:, b, :], f32(val_hi[:, b, :]), ALU.subtract).then_inc(val_lo_ready, 1)
            dve.wait_ge(cd_psum, 1)
            nc.vector.tensor_copy(score_c[:, :, 0:S], psT[:, 0, 0:BS].rearrange("p (b s) -> p b s", b=B))
            dve.wait_ge(cd_psum, 2)
            nc.vector.tensor_copy(score_d[:], psT[:, 1, 0:BS].rearrange("p (b s) -> p b s", b=B)).then_inc(cd_ready, 1)
            for k in range(KD):
                dve.wait_ge(m_hi, k + 1)
                src = (psA[:, 0], psA[:, 1], psO[:, 0], psO[:, 1])[k]
                dst = slice(SCORE_AT[k], SCORE_AT[k] + S)
                nc.vector.tensor_tensor(proj_lo[:, :, dst], src[:, 0:BS].rearrange("p (b s) -> p b s", b=B),
                                        f32(proj_hi[:, :, dst]), ALU.subtract).then_inc(m_lo, 1)
            dve.wait_ge(m_lo, KD)
            dve.wait_ge(cd_ready, 1)

            def lo_part(b, i, t):
                wait_if_positive(dve, x_hi_ready, T, i, T * b + t + 1)
                nc.vector.tensor_tensor(x_lo[:, b % 2, t, :], psT[:, t, :], f32(x_hi[:, b % 2, t, :]),
                                        ALU.subtract).then_inc(x_lo_ready, 1)

            def quadratic(b, i, t, lag):
                q = (b - lag) % B
                wait_if_positive(dve, proj_psum, T, i, T * (b - lag) + t + 1)
                nc.vector.tensor_tensor(sc[:, q, t, :], psA[:, t, YW:YW + SW], score_c[:, q, :], ALU.add).then_inc(sc_ready, 1)
                wait_if_positive(dve, quad_ready, T, i, T * (b - lag - 1) + t + 1)
                nc.vector.tensor_tensor_reduce(out=waste_dve[:, 2 * t, 0:YW], in0=psA[:, t, 0:YW], in1=xs[:, q, t, P:D],
                                               scale=1.0, scalar=0.0, op0=ALU.mult, op1=ALU.add,
                                               accum_out=quad_a[:, q, t:t + 1])
                wait_if_positive(dve, sc_ready, T, i, T * (b - lag) + t + 1)
                nc.vector.tensor_tensor_reduce(out=waste_dve[:, 2 * t + 1, 0:P], in0=psB[:, 0:P], in1=xs[:, q, t, 0:P],
                                               scale=1.0, scalar=sc[:, q, t, LIN:LIN + 1], op0=ALU.mult, op1=ALU.add,
                                               accum_out=quad_b[:, q, t:t + 1]).then_inc(quad_ready, 1)

            def residual(b, i, t):
                q = (b - 3) % B
                wait_if_positive(dve, mix_psum, T, i, T * (b - 3) + t + 1)
                wait_if_positive(dve, inv_ready, 1, i, b - 2)
                nc.vector.scalar_tensor_tensor(hid[:, (b - 3) % 2, t, :], psO[:, t, :], inv_sum[:, q, t:t + 1],
                                               xs[:, q, t, :], ALU.mult, ALU.add).then_inc(hid_ready, 1)

            def body(b, i, live):
                if live(2):
                    q = (b - 2) % B
                    quadratic(b, i, 1, 2)
                    wait_if_positive(dve, quad_ready, T, i, T * (b - 2) + T)
                    nc.vector.tensor_tensor(var[:, q, :], quad_a[:, q, :], quad_b[:, q, :], ALU.add).then_inc(var_sum, 1)
                if live(3):
                    residual(b, i, 0)
                if live(2):
                    wait_if_positive(dve, var_sum, 1, i, b - 1)
                    nc.vector.tensor_scalar(var[:, q, :], var[:, q, :], EPS, None, ALU.max).then_inc(var_ready, 1)
                if live(0):
                    lo_part(b, i, 0)
                if live(2):
                    wait_if_positive(dve, rstd_ready, 1, i, b - 1)
                    wait_if_positive(dve, prob_ready, T, i, T * (b - 4) + T)
                    for t in range(T):
                        nc.vector.scalar_tensor_tensor(logits[:, b % 2, t, :], sc[:, q, t, 0:S], rstd[:, q, t:t + 1],
                                                       score_d[:, q, :], ALU.mult, ALU.add).then_inc(logits_ready, 1)
                    wait_if_positive(dve, logits_ready, T, i, T * (b - 2) + T)
                    nc.vector.reduce_max(neg_max[:, q, :], logits[:, b % 2, :, :], axis=AX_X, negate=True).then_inc(max_ready, 1)
                if live(3):
                    residual(b, i, 1)
                if live(2):
                    wait_if_positive(dve, prob_ready, T, i, T * (b - 2) + T)
                    nc.vector.reciprocal(inv_sum[:, q, :], prob_sum[:, q, :]).then_inc(inv_ready, 1)
                if live(1):
                    quadratic(b, i, 0, 1)
                if live(0):
                    lo_part(b, i, 1)
                if live(2):
                    wait_if_positive(dve, prob_hi_ready, 1, i, b - 1)
                    nc.vector.tensor_tensor(prob_lo[:, b % 2, :], psE[0:S, 0:T * P], f32(prob_hi[:, b % 2, :]),
                                            ALU.subtract).then_inc(prob_lo_ready, 1)

            pipeline(dve, body)

        @block.tensor
        def _(pe):
            pe.wait_ge(ident_ready, 1)
            pe.wait_ge(ctx_loaded, 16)
            for k in range(KA):
                for b in range(B):
                    last = nc.tensor.transpose((psA[:, 0], psA[:, 1], psB)[k][:, b * S:(b + 1) * S],
                                               cx[:, b, k * P:(k + 1) * P], ident[0:S, 0:S])
                last.then_inc(cxT_psum, 1)
            pe.wait_ge(vec_loaded, 64)
            nc.tensor.transpose(psE[:, 0:4 * KH], vec_rows[:], ident[0:4 * KH, 0:4 * KH]).then_inc(vec_psum, 1)
            pe.wait_ge(wa_loaded, 16)
            pe.wait_ge(cxT_ready, KA)
            for k in range(KH):
                dst = (psT[:, 0], psT[:, 1], psO[:, 0], psO[:, 1])[k]
                for j in range(KA):
                    last = nc.tensor.matmul(dst[:, 0:BS], wa[:, j, k * P:(k + 1) * P], cxT[:, j, :],
                                            start=(j == 0), stop=(j == KA - 1))
                last.then_inc(vT_psum, 1)
            pe.wait_ge(wc_ready, KD)
            for k in range(KH):
                if k >= 2:
                    pe.wait_ge(vT_ready, k + 1)
                dst = (psA[:, 0], psA[:, 1], psO[:, 0], psO[:, 1])[k]
                for j in range(KD):
                    last = nc.tensor.transpose(dst[:, j * P:(j + 1) * P], wt[:, j, k * P:(k + 1) * P], ident[:])
                last.then_inc(wtT_psum, 1)
            pe.wait_ge(bc_ready, 1)
            pe.wait_ge(vec_ready, 1)
            for k in range(KH):
                last = nc.tensor.transpose(psB[:, k * P:(k + 1) * P], bt_rows[:, k * P:(k + 1) * P], ident[:])
            last.then_inc(rowsT_psum, 1)
            pe.wait_ge(beta1_loaded, 16)
            for k in range(KH):
                last = nc.tensor.transpose(psE[:, k * P:(k + 1) * P], beta1_rows[:, k * P:(k + 1) * P], ident[:])
            last.then_inc(rowsT_psum, 1)
            pe.wait_ge(ones_ready, 1)
            pe.wait_ge(vT_ready, KH)
            for k in range(KH):
                last = nc.tensor.matmul(psT[:, 0, 0:BS], mean_of, vT[:, k, :], start=(k == 0), stop=(k == KH - 1))
            last.then_inc(mean_psum, 1)
            pe.wait_ge(wtT_ready, KH)
            for k in range(KD):
                dst = (psA[:, 0], psA[:, 1], psO[:, 0], psO[:, 1])[k]
                for h in range(KH):
                    last = nc.tensor.matmul(dst[:, 0:D - k * P], wtT[:, h, k * P:(k + 1) * P], wtT[:, h, k * P:D],
                                            start=(h == 0), stop=(h == KH - 1))
                last.then_inc(g_psum, 1)
                if k == 1:
                    pe.wait_ge(ksq_ready, KH)
                    for h in range(KH):
                        last = nc.tensor.matmul(psT[:, 1, 0:BS], mean_of, kSq[:, h, :], start=(h == 0), stop=(h == KH - 1))
                    last.then_inc(kvar_psum, 1)
            pe.wait_ge(wo_ready, KH)
            pe.wait_ge(rowsT_ready, 1)
            for b in range(B):
                if b >= 2:
                    pe.wait_ge(val_ready, b - 1)
                dst = (psB, psE)[b % 2]
                for h in range(KH):
                    last = nc.tensor.matmul(dst[0:S, :], vT[:, h, b * S:(b + 1) * S], wo[:, h, :],
                                            start=(h == 0), stop=(h == KH - 1))
                last.then_inc(val_psum, 1)
            pe.wait_ge(kT_ready, KH)
            pe.wait_ge(kvar_ready, 1)
            for n, rows in enumerate((btT, beta1T)):
                for h in range(KH):
                    last = nc.tensor.matmul(psT[:, n, 0:BS], rows[:, h, :], kT[:, h, :], start=(h == 0), stop=(h == KH - 1))
                last.then_inc(cd_psum, 1)
            pe.wait_ge(wgT_ready, KH)
            for k in range(KD):
                pe.wait_ge(g_lo, k + 1)
                dst = (psA[:, 0], psA[:, 1], psO[:, 0], psO[:, 1])[k]
                for h in range(KH):
                    last = nc.tensor.matmul(dst[:, 0:BS], wgT[:, h, k * P:(k + 1) * P], kT[:, h, :],
                                            start=(h == 0), stop=(h == KH - 1))
                last.then_inc(m_psum, 1)
            pe.wait_ge(cd_ready, 1)
            pe.wait_ge(m_lo, KD)
            pe.wait_ge(val_lo_ready, B)

            def transpose_x(b, i, t):
                pe.wait_ge(x_loaded[b][t], 16 * (i + 1))
                wait_if_positive(pe, x_lo_ready, T, i, T * (b - 1) + t + 1)
                for k in range(KD):
                    last = nc.tensor.transpose(psT[:, t, k * P:(k + 1) * P], xs[:, b, t, k * P:(k + 1) * P], ident[:])
                last.then_inc(xT_psum, 1)

            PASSES = [(a, w, k) for k in range(KD) for a, w in ((x_hi, proj_hi), (x_hi, proj_lo), (x_lo, proj_hi))]

            def project(b, i, t, first, count):
                q, par = (b - 1) % B, (b - 1) % 2
                if first == 0:
                    wait_if_positive(pe, x_lo_ready, T, i, T * (b - 1) + t + 1)
                    wait_if_positive(pe, quad_ready, T, i, T * (b - 2) + t + 1)
                for n in range(first, first + count):
                    part, w, k = PASSES[n]
                    skip = 0 if k == 0 else (k - 1) * P
                    nc.tensor.matmul(psA[:, t, skip:YW + SW], part[:, par, t, k * P:(k + 1) * P],
                                     w[:, q, OFFSET[k]:OFFSET[k] + WIDTH[k]], start=(n == 0), stop=(n == len(PASSES) - 1))

            def project_diagonal(b, i, t):
                q, par = (b - 1) % B, (b - 1) % 2
                wait_if_positive(pe, quad_ready, T, i, T * (b - 1) + t)
                for n in range(3):
                    part, w, _ = PASSES[n]
                    last = nc.tensor.matmul(psB[:, 0:P], part[:, par, t, 0:P], w[:, q, DIAG0:DIAG0 + P],
                                            start=(n == 0), stop=(n == 2))
                last.then_inc(proj_psum, 1)

            def body(b, i, live):
                half = len(PASSES) // 2
                if live(0):
                    transpose_x(b, i, 0)
                if live(1):
                    project(b, i, 0, 0, len(PASSES))
                    project_diagonal(b, i, 0)
                if live(0):
                    transpose_x(b, i, 1)
                if live(1):
                    project(b, i, 1, 0, half)
                if live(2):
                    wait_if_positive(pe, prob_ready, T, i, T * (b - 2) + T)
                    wait_if_positive(pe, prob_lo_ready, 1, i, b - 2)
                    for t in range(T):
                        last = nc.tensor.transpose(psE[0:S, t * P:(t + 1) * P], prob[:, b % 2, t, :], ident[:])
                    last.then_inc(probT_psum, 1)
                if live(1):
                    project(b, i, 1, half, len(PASSES) - half)
                    project_diagonal(b, i, 1)
                if live(2):
                    q = (b - 2) % B
                    wait_if_positive(pe, prob_lo_ready, 1, i, b - 1)
                    for t in range(T):
                        wait_if_positive(pe, hid_ready, T, i, T * (b - 3) + t + 1)
                        for n, (pr, v) in enumerate(((prob_hi, val_hi), (prob_hi, val_lo), (prob_lo, val_hi))):
                            last = nc.tensor.matmul(psO[:, t, :], pr[:, b % 2, t * P:(t + 1) * P], v[:, q, :],
                                                    start=(n == 0), stop=(n == 2))
                        last.then_inc(mix_psum, 1)

            pipeline(pe, body)


_PRE = "L0_xattn_"
_INS = ["x", "ctx_768"] + [_PRE + n for n in ("W_text", "b_text", "W_audio", "b_audio", "W_out", "b_out",
                                              "g1", "beta1", "g2", "beta2", "g_out", "beta_out")]


def kernel(**inputs):
    import numpy as _np
    import concourse.bacc as _bacc
    from concourse import mybir as _mybir
    from concourse.bass_utils import run_bass_kernel_spmd as _run

    nc = _bacc.Bacc("TRN2", target_bir_lowering=False, num_devices=1)
    arrays, args = {}, []
    for name in _INS:
        a = _np.ascontiguousarray(inputs[name])
        arrays[f"in_{name}_dram"] = a
        args.append(nc.dram_tensor(f"in_{name}_dram", a.shape, _mybir.dt.from_np(a.dtype), kind="ExternalInput").ap())
    shape = inputs["x"].shape
    args.append(nc.dram_tensor("out_dram", shape, _mybir.dt.float32, kind="ExternalOutput").ap())
    cross_attention(nc, *args)
    r = _run(nc, [arrays], core_ids=[0])
    return r.results[0]["out_dram"]
```

```python
from contextlib import ExitStack

import concourse.bass as bass
from concourse import mybir

F32 = mybir.dt.float32
F32R = mybir.dt.float32r
ALU = mybir.AluOpType
ACT = mybir.ActivationFunctionType
AX_X = mybir.AxisListType.X

P = 128
EPS = 1e-5


def cross_attention(nc, x, ctx, w_text, b_text, w_audio, b_audio, w_out, b_out,
                    g1, beta1, g2, beta2, g_out, beta_out, out):
    B, L, D = x.shape
    _, S, DA = ctx.shape
    H = w_text.shape[1]
    KD, KA, KH = D // P, DA // P, H // P
    SCALE = float(H) ** -0.5
    assert D == H == 4 * P and DA % P == 0 and S < P

    T = 2
    ROWS = T * P
    STEPS = B * L // ROWS
    PER_BATCH = L // ROWS
    BS = B * S
    KEYS = [(at, min(P, BS - at)) for at in range(0, BS, P)]
    SW = S + 3
    LIN, NXBAR = S, S + 1
    YW = D - P
    WIDTH = [YW + SW] + [D - k * P + SW for k in range(1, KD)]
    OFFSET = [0, WIDTH[0] + P] + [WIDTH[0] + P + sum(WIDTH[1:k]) for k in range(2, KD)]
    DIAG0 = WIDTH[0]
    COLS = sum(WIDTH) + P
    SCORE_AT = [OFFSET[k] + WIDTH[k] - SW for k in range(KD)]

    with ExitStack() as stack:
        def sb(name, shape, dt=F32):
            return stack.enter_context(nc.sbuf_tensor(name, shape, dt))

        def sem(name):
            return stack.enter_context(nc.semaphore(name))

        psT = stack.enter_context(nc.psum_tensor("psT", [P, T, 512], F32))
        psA = stack.enter_context(nc.psum_tensor("psA", [P, T, 512], F32))
        psB = stack.enter_context(nc.psum_tensor("psB", [P, 512], F32))
        psE = stack.enter_context(nc.psum_tensor("psE", [P, 512], F32))
        psO = stack.enter_context(nc.psum_tensor("psO", [P, T, 512], F32))

        ident = sb("ident", [P, P])
        proj_hi = sb("proj_hi", [P, B, COLS], F32R)
        proj_lo = sb("proj_lo", [P, B, COLS], F32R)
        val_hi = sb("val_hi", [S, B, H], F32R)
        val_lo = sb("val_lo", [S, B, H], F32R)
        score_c = sb("score_c", [P, B, SW])
        score_d = sb("score_d", [P, B, S])
        gain = sb("gain", [P, H])
        shift = sb("shift", [P, H])
        neg_half = sb("neg_half", [P, 4])
        eps_sum = sb("eps_sum", [P, T])
        xs = sb("xs", [P, B, T, D])
        x_hi = sb("x_hi", [P, 2, T, D], F32R)
        x_lo = sb("x_lo", [P, 2, T, D], F32R)
        sc = sb("sc", [P, B, T, SW])
        quad_a = sb("quad_a", [P, B, T])
        quad_b = sb("quad_b", [P, B, T])
        var = sb("var", [P, B, T])
        rstd = sb("rstd", [P, B, T])
        logits = sb("logits", [P, 2, T, S])
        neg_max = sb("neg_max", [P, B, T])
        prob = sb("prob", [P, 2, T, S])
        prob_sum = sb("prob_sum", [P, B, T])
        inv_sum = sb("inv_sum", [P, B, T])
        prob_hi = sb("prob_hi", [S, 2, T * P], F32R)
        prob_lo = sb("prob_lo", [S, 2, T * P], F32R)
        hid = sb("hid", [P, 2, T, H])
        sq_sum = sb("sq_sum", [P, B, T])
        var2 = sb("var2", [P, B, T])
        rstd2 = sb("rstd2", [P, B, T])
        shift2 = sb("shift2", [P, B, T])
        zs = sb("zs", [P, B, T, H])
        waste_dve = sb("waste_dve", [P, 4, H], mybir.dt.bfloat16)
        waste_act = sb("waste_act", [P, 2, H], mybir.dt.bfloat16)

        vec_rows = sb("vec_rows", [4 * KH, P])
        vec_cols = sb("vec_cols", [P, 4 * KH])
        g1s = sb("g1s", [P, KH])
        bt_rows = sb("bt_rows", [P, H])
        beta1_rows = sb("beta1_rows", [P, H])
        bo_rows = sb("bo_rows", [P, H])
        btT_hi = sb("btT_hi", [P, KH, P], F32R)
        btT_lo = sb("btT_lo", [P, KH, P], F32R)
        beta1T = sb("beta1T", [P, KH, P])
        sums = sb("sums", [P, 16])
        osums = sb("osums", [P, KH + 1])
        lin = sb("lin", [P, KD])
        wa = sb("wa", [P, KA, H])
        cxT = sb("cxT", [P, KA, BS])
        vT = sb("vT", [P, KH, BS])
        vT_hi = sb("vT_hi", [P, KH, BS], F32R)
        vT_lo = sb("vT_lo", [P, KH, BS], F32R)
        kg_hi = sb("kg_hi", [P, KH, BS], F32R)
        kg_lo = sb("kg_lo", [P, KH, BS], F32R)
        wo_hi = sb("wo_hi", [P, KH, H], F32R)
        wo_lo = sb("wo_lo", [P, KH, H], F32R)
        kvar = sb("kvar", [P, 4])
        krstd = sb("krstd", [P, 4])
        room = [zs[:].rearrange("p b t h -> p (b t h)"), hid[:].rearrange("p c t h -> p (c t h)")]
        used = [0, 0]

        def borrow(where, n):
            used[where] += n
            assert used[where] <= room[where].shape[1]
            return room[where][:, used[where] - n:used[where]]

        values = borrow(0, B * H)
        vbuf = values.rearrange("p (b h) -> p b h", b=B)[0:S]
        cx = values[:, 0:B * DA].rearrange("p (b d) -> p b d", b=B)[0:S]
        kSq = borrow(0, KH * BS).rearrange("p (k n) -> p k n", k=KH)
        kSqSum = borrow(0, BS)
        kT = borrow(1, KH * BS).rearrange("p (k n) -> p k n", k=KH)
        mean_of = borrow(1, P)
        ones = borrow(1, P)
        diag = borrow(1, BS)
        wt = xs[:, 0:2].rearrange("p b t d -> p (b t) d")
        wo = xs[:, 2:4].rearrange("p b t d -> p (b t) d")
        wtT_hi = x_hi[:].rearrange("p c t d -> p (c t) d")
        wtT_lo = x_lo[:].rearrange("p c t d -> p (c t) d")

        wt_loaded = [sem(f"wt_loaded{n}") for n in range(2)]
        wa_loaded, wo_loaded = sem("wa_loaded"), sem("wo_loaded")
        ctx_loaded, vec_loaded = sem("ctx_loaded"), sem("vec_loaded")
        bt_loaded, beta1_loaded, bo_loaded = sem("bt_loaded"), sem("beta1_loaded"), sem("bo_loaded")
        gs_loaded, t_copied = sem("gs_loaded"), sem("t_copied")
        ident_ready, ones_ready, gain_ready = sem("ident_ready"), sem("ones_ready"), sem("gain_ready")
        cxT_psum, cxT_ready = sem("cxT_psum"), sem("cxT_ready")
        vec_psum, vec_ready = sem("vec_psum"), sem("vec_ready")
        g1s_ready = sem("g1s_ready")
        vT_psum, vT_ready, vT_hi_ready, vT_lo_ready = sem("vT_psum"), sem("vT_ready"), sem("vT_hi_ready"), sem("vT_lo_ready")
        wsum_act, wc_ready, wtT_psum = sem("wsum_act"), sem("wc_ready"), sem("wtT_psum")
        wtT_hi_ready, wtT_lo_ready, lin_ready = sem("wtT_hi_ready"), sem("wtT_lo_ready"), sem("lin_ready")
        bc_ready, rowsT_psum, rowsT_ready, btT_hi_ready = sem("bc_ready"), sem("rowsT_psum"), sem("rowsT_ready"), sem("btT_hi_ready")
        g_psum, g_hi, g_lo = sem("g_psum"), sem("g_hi"), sem("g_lo")
        mean_psum, kc_ready, ksq_ready, kvar_psum = sem("mean_psum"), sem("kc_ready"), sem("ksq_ready"), sem("kvar_psum")
        ksqsum_ready, diag_ready, krows_psum = sem("ksqsum_ready"), sem("diag_ready"), sem("krows_psum")
        kvar_ready, krstd_ready, kn_ready, kT_ready = sem("kvar_ready"), sem("krstd_ready"), sem("kn_ready"), sem("kT_ready")
        kg_hi_ready, kg_lo_ready = sem("kg_hi_ready"), sem("kg_lo_ready")
        osums_ready, wo_hi_ready, wo_ready, bo_ready = sem("osums_ready"), sem("wo_hi_ready"), sem("wo_ready"), sem("bo_ready")
        val_psum, val_ready, val_hi_ready, val_lo_ready = sem("val_psum"), sem("val_ready"), sem("val_hi_ready"), sem("val_lo_ready")
        m_psum, m_hi, m_lo, cd_psum, cd_ready = sem("m_psum"), sem("m_hi"), sem("m_lo"), sem("cd_psum"), sem("cd_ready")
        extras_ready, lin_hi_ready, lin_lo_ready = sem("extras_ready"), sem("lin_hi_ready"), sem("lin_lo_ready")
        dve_own, pool_own, act_own = sem("dve_own"), sem("pool_own"), sem("act_own")

        W_BANK = (psT[:, 0], psT[:, 1], psO[:, 0], psO[:, 1])
        V_BANK = (psA[:, 0], psA[:, 1], psB[:], psE[:])
        VAL_BANK = (psB[:], psE[:], psB[:], psA[:, 1])
        M_BANK = (psO[:, 0], psO[:, 1], psE[:], psB[:])
        T_PARTS = [(0, DIAG0, P), (0, 0, YW)] + [(k, OFFSET[k], D - k * P) for k in range(1, KD)]

        x_loaded = [[sem(f"x_loaded{b}{t}") for t in range(T)] for b in range(B)]
        out_stored = [sem(f"out_stored{b}") for b in range(B)]
        xT_psum, x_hi_ready, x_lo_ready = sem("xT_psum"), sem("x_hi_ready"), sem("x_lo_ready")
        proj_psum, sc_ready, quad_ready = sem("proj_psum"), sem("sc_ready"), sem("quad_ready")
        var_sum, var_ready, rstd_ready = sem("var_sum"), sem("var_ready"), sem("rstd_ready")
        logits_ready = sem("logits_ready")
        max_ready = sem("max_ready")
        prob_ready = sem("prob_ready")
        inv_ready, probT_psum = sem("inv_ready"), sem("probT_psum")
        prob_hi_ready, prob_lo_ready = sem("prob_hi_ready"), sem("prob_lo_ready")
        mix_psum, hid_ready, sq_ready = sem("mix_psum"), sem("hid_ready"), sem("sq_ready")
        var2_ready, rstd2_ready, shift2_ready = sem("var2_ready"), sem("rstd2_ready"), sem("shift2_ready")
        z_ready, zg_ready, out_ready = sem("z_ready"), sem("zg_ready"), sem("out_ready")

        f32 = lambda ap: ap.bitcast(F32)

        def pipeline(eng, body):
            for b in range(1, B):
                body(b, 0, lambda lag, b=b: b - lag >= 0)
            with eng.Fori(1, STEPS // B) as i:
                for b in range(B):
                    body(b, i, lambda lag: True)
            for b in range(B):
                body(b, STEPS // B, lambda lag, b=b: b - lag < 0)

        def wait_if_positive(eng, s, per, i, const):
            value = per * B * i + const
            if isinstance(i, int) and value <= 0:
                return
            eng.wait_ge(s, value)

        block = stack.enter_context(nc.Block())

        @block.sync
        def _(sp):
            sp.dma_start(cx, ctx.rearrange("b s d -> s b d")).then_inc(ctx_loaded, 16)
            wt_rows = w_text.rearrange("(k p) h -> p k h", p=P)
            for n in range(2):
                sp.dma_start(wt[:, 2 * n:2 * n + 2, :], wt_rows[:, 2 * n:2 * n + 2, :]).then_inc(wt_loaded[n], 16)
            sp.dma_start(wa[:], w_audio.rearrange("(k p) h -> p k h", p=P)).then_inc(wa_loaded, 16)
            sp.dma_start(wo, w_out.rearrange("(k p) h -> p k h", p=P)).then_inc(wo_loaded, 16)

            def body(b, i, live):
                if live(0):
                    if isinstance(i, int) and i == 0:
                        if b == 0:
                            sp.wait_ge(wtT_psum, KH)
                            sp.wait_ge(lin_ready, KD)
                        if b == 2:
                            for part, (k, at, n) in enumerate(T_PARTS):
                                for buf, made in ((proj_hi, g_hi), (proj_lo, g_lo)):
                                    sp.wait_ge(made, part + 1)
                                    one = f32(buf[:, 0:1, at:at + n])
                                    sp.dma_start(f32(buf[:, 1:B, at:at + n]), one.to_broadcast([P, B - 1, n])).then_inc(t_copied, 16)
                            sp.wait_ge(wo_ready, KH)
                    for t in range(T):
                        wait_if_positive(sp, hid_ready, T, i, T * (b - B) + t + 1)
                        src = x[b, bass.ds(i * ROWS, ROWS), :].rearrange("(p t) d -> p t d", t=T)[:, t, :]
                        sp.dma_start(xs[:, b, t, :], src).then_inc(x_loaded[b][t], 16)
                if live(5):
                    q, j = (b - 5) % B, i + (b - 5) // B
                    wait_if_positive(sp, out_ready, T, i, T * (b - 5) + T)
                    dst = out[q, bass.ds(j * ROWS, ROWS), :].rearrange("(p t) d -> p t d", t=T)
                    sp.dma_start(dst, zs[:, q, :, :]).then_inc(out_stored[q], 16)

            for b in range(B):
                body(b, 0, lambda lag, b=b: b - lag >= 0)
            for b in range(B):
                body(b, 1, lambda lag, b=b: B + b - lag >= 0)
            with sp.Fori(2, STEPS // B) as i:
                for b in range(B):
                    body(b, i, lambda lag: True)
            for k in range(2):
                for b in range(B):
                    body(b, STEPS // B + k, lambda lag, s=k * B + b: lag > 0 and s - lag < 0)
            for b in range(B):
                sp.wait_ge(out_stored[b], 16 * PER_BATCH)

        @block.gpsimd
        def _(pool):
            nc.gpsimd.memset(ident[:], 1.0).then_inc(pool_own, 1)
            nc.gpsimd.memset(mean_of, 1.0 / H).then_inc(ones_ready, 1)
            nc.gpsimd.memset(ones, 1.0).then_inc(ones_ready, 1)
            nc.gpsimd.memset(neg_half[:], -0.5).then_inc(pool_own, 1)
            nc.gpsimd.memset(eps_sum[:], H * EPS).then_inc(pool_own, 1)
            pool.wait_ge(pool_own, 1)
            nc.gpsimd.affine_select(out=ident[:], in_=ident[:], compare_op=ALU.is_equal, fill=0.0, base=0,
                                    pattern=[[-1, P]], channel_multiplier=1).then_inc(ident_ready, 1)
            nc.gpsimd.memset(score_c[:, :, S:SW], 0.0).then_inc(extras_ready, 1)
            for buf in (proj_hi, proj_lo):
                for k in range(KD):
                    at = SCORE_AT[k]
                    nc.gpsimd.memset(f32(buf[:, :, at + S:at + SW]), 0.0).then_inc(pool_own, 1)
            pool.wait_ge(pool_own, 3 + 2 * KD)
            for k in range(KD):
                at = SCORE_AT[k] + NXBAR
                nc.gpsimd.memset(f32(proj_hi[:, :, at:at + 1]), -1.0 / D).then_inc(extras_ready, 1)
            pool.wait_ge(osums_ready, 1)
            nc.gpsimd.tensor_scalar(bo_rows[:], bo_rows[:], 1.0, osums[:, KH:KH + 1], ALU.mult, ALU.add).then_inc(bo_ready, 1)
            for k in range(KH):
                pool.wait_ge(vT_hi_ready, k + 1)
                nc.gpsimd.tensor_tensor(vT_lo[:, k, :], vT[:, k, :], f32(vT_hi[:, k, :]), ALU.subtract).then_inc(vT_lo_ready, 1)
            pool.wait_ge(kvar_ready, 1)
            nc.gpsimd.tensor_tensor(krstd[:, 0:3], kvar[:, 0:3], neg_half[:, 0:3], ALU.pow).then_inc(krstd_ready, 1)
            pool.wait_ge(gs_loaded, 32)
            nc.gpsimd.tensor_scalar(gain[:], gain[:], float(H) ** 0.5, 0.0, ALU.mult, ALU.add).then_inc(gain_ready, 1)
            pool.wait_ge(gain_ready, 1)

            def body(b, i, live):
                if live(2):
                    q = (b - 2) % B
                    wait_if_positive(pool, var_ready, 1, i, b - 1)
                    nc.gpsimd.tensor_tensor(rstd[:, q, :], var[:, q, :], neg_half[:, 0:T], ALU.pow).then_inc(rstd_ready, 1)
                if live(4):
                    q = (b - 4) % B
                    for t in range(T):
                        wait_if_positive(pool, z_ready, T, i, T * (b - 4) + t + 1)
                        nc.gpsimd.tensor_tensor(zs[:, q, t, :], zs[:, q, t, :], gain[:], ALU.mult).then_inc(zg_ready, 1)
                if live(3):
                    q = (b - 3) % B
                    wait_if_positive(pool, sq_ready, T, i, T * (b - 3) + T)
                    nc.gpsimd.tensor_tensor(var2[:, q, :], sq_sum[:, q, :], eps_sum[:], ALU.add).then_inc(var2_ready, 1)
                    wait_if_positive(pool, var2_ready, 1, i, b - 2)
                    nc.gpsimd.tensor_tensor(rstd2[:, q, :], var2[:, q, :], neg_half[:, 0:T], ALU.pow).then_inc(rstd2_ready, 1)
                    wait_if_positive(pool, rstd2_ready, 1, i, b - 2)
                    nc.gpsimd.tensor_tensor(shift2[:, q, :], sc[:, q, :, NXBAR], rstd2[:, q, :], ALU.mult).then_inc(shift2_ready, 1)
                if live(4):
                    q = (b - 4) % B
                    for t in range(T):
                        wait_if_positive(pool, zg_ready, T, i, T * (b - 4) + t + 1)
                        nc.gpsimd.tensor_tensor(zs[:, q, t, :], zs[:, q, t, :], shift[:], ALU.add).then_inc(out_ready, 1)

            pipeline(pool, body)

        @block.scalar
        def _(act):
            for n, v in enumerate((g1, g2, beta2, b_audio)):
                act.dma_start(vec_rows[n * KH:(n + 1) * KH, :], v.rearrange("(k p) -> k p", p=P)).then_inc(vec_loaded, 16)

            def load_row(row, v, loaded):
                act.dma_start(row[:], v.rearrange("(a h) -> a h", a=1).to_broadcast([P, H])).then_inc(loaded, 16)

            load_row(bt_rows, b_text, bt_loaded)
            act.wait_ge(ones_ready, 1)
            nc.scalar.activation(waste_act[:, 0, 0:1], mean_of[:, 0:1], ACT.Exp).then_inc(act_own, 1)
            for k in range(KA):
                act.wait_ge(cxT_psum, k + 1)
                nc.scalar.activation(cxT[:, k, :], V_BANK[k][:, 0:BS], ACT.Copy).then_inc(cxT_ready, 1)
            load_row(beta1_rows, beta1, beta1_loaded)
            load_row(bo_rows, b_out, bo_loaded)
            load_row(gain, g_out, gs_loaded)
            load_row(shift, beta_out, gs_loaded)
            for n, k in enumerate((1, 3)):
                act.wait_ge(wt_loaded[n], 16)
                act.wait_ge(act_own, n + 1)
                nc.scalar.activation(waste_act[:, 0, :], wt[:, k, :], ACT.Copy, scale=-1.0 / H,
                                     accum_out=sums[:, k:k + 1]).then_inc(act_own, 1)
                wsum_done = n + 2
            for k in range(KH):
                act.wait_ge(wtT_psum, k + 1)
                nc.scalar.activation(wtT_hi[:, k, :], W_BANK[k], ACT.Copy).then_inc(wtT_hi_ready, 1)
            act.wait_ge(vec_ready, 1)
            for k in range(KH):
                act.wait_ge(vT_psum, k + 1)
                nc.scalar.activation(vT[:, k, :], V_BANK[k][:, 0:BS], ACT.Identity,
                                     bias=vec_cols[:, 3 * KH + k:3 * KH + k + 1]).then_inc(vT_ready, 1)
            act.wait_ge(wo_loaded, 16)
            act.wait_ge(bo_loaded, 16)
            for k in range(KH + 1):
                row = wo[:, k, :] if k < KH else bo_rows[:]
                act.wait_ge(act_own, wsum_done + max(k - 1, 0))
                last = nc.scalar.activation(waste_act[:, k % 2, :], row, ACT.Copy, scale=-1.0 / H, accum_out=osums[:, k:k + 1])
                last.then_inc(act_own if k < KH else osums_ready, 1)

            def t_hi(parts):
                for k, at, n in parts:
                    act.wait_ge(g_psum, k + 1)
                    if k == 0:
                        skip = 0 if at == DIAG0 else P
                        nc.scalar.activation(proj_hi[:, 0, at:at + n], W_BANK[k][:, skip:skip + n], ACT.Copy,
                                             scale=(1.0 if at == DIAG0 else 2.0) / H).then_inc(g_hi, 1)
                    else:
                        last = nc.scalar.activation(proj_hi[:, 0, at:at + P], W_BANK[k][:, 0:P], ACT.Copy, scale=1.0 / H)
                        if n > P:
                            last = nc.scalar.activation(proj_hi[:, 0, at + P:at + n], W_BANK[k][:, P:n], ACT.Copy, scale=2.0 / H)
                        last.then_inc(g_hi, 1)

            t_hi(T_PARTS[0:2])
            for k in range(KH):
                act.wait_ge(kc_ready, k + 1)
                nc.scalar.activation(kSq[:, k, :], kT[:, k, :], ACT.Square).then_inc(ksq_ready, 1)
            t_hi(T_PARTS[2:])
            act.wait_ge(rowsT_psum, 1)
            nc.scalar.activation(btT_hi[:], psB[:], ACT.Copy).then_inc(btT_hi_ready, 1)
            act.wait_ge(rowsT_psum, 2)
            nc.scalar.activation(beta1T[:], psE[:], ACT.Copy, scale=SCALE).then_inc(rowsT_ready, 1)

            def value_hi(b):
                act.wait_ge(val_ready, b + 1)
                nc.scalar.activation(val_hi[:, b, :], vbuf[:, b, :], ACT.Copy).then_inc(val_hi_ready, 1)

            for k in range(KH):
                act.wait_ge(kn_ready, k + 1)
                nc.scalar.activation(kT[:, k, :], kT[:, k, :], ACT.Identity,
                                     bias=vec_cols[:, 2 * KH + k:2 * KH + k + 1]).then_inc(kT_ready, 1)
                if k >= 1:
                    act.wait_ge(kT_ready, k)
                    nc.scalar.activation(kg_hi[:, k - 1, :], kT[:, k - 1, :], ACT.Copy, scale=g1s[:, k - 1:k]).then_inc(kg_hi_ready, 1)
            act.wait_ge(kT_ready, KH)
            nc.scalar.activation(kg_hi[:, KH - 1, :], kT[:, KH - 1, :], ACT.Copy, scale=g1s[:, KH - 1:KH]).then_inc(kg_hi_ready, 1)
            for b in range(3):
                value_hi(b)
            for k in range(KD):
                act.wait_ge(m_psum, k + 1)
                nc.scalar.activation(proj_hi[:, :, SCORE_AT[k]:SCORE_AT[k] + S],
                                     M_BANK[k][:, 0:BS].rearrange("p (b s) -> p b s", b=B), ACT.Copy).then_inc(m_hi, 1)

            def hi_part(b, i, t):
                wait_if_positive(act, xT_psum, T, i, T * b + t + 1)
                wait_if_positive(act, proj_psum, T, i, T * (b - 2) + t + 1)
                nc.scalar.activation(x_hi[:, b % 2, t, :], psT[:, t, :], ACT.Copy).then_inc(x_hi_ready, 1)

            def square(b, i, t):
                q = (b - 3) % B
                wait_if_positive(act, hid_ready, T, i, T * (b - 3) + t + 1)
                wait_if_positive(act, sq_ready, T, i, T * (b - 4) + t + 1)
                nc.scalar.activation(waste_act[:, t, :], hid[:, (b - 3) % 2, t, :], ACT.Square,
                                     bias=sc[:, q, t, NXBAR:NXBAR + 1],
                                     accum_out=sq_sum[:, q, t:t + 1]).then_inc(sq_ready, 1)

            def body(b, i, live):
                if live(0):
                    hi_part(b, i, 0)
                if live(3):
                    square(b, i, 0)
                if live(2):
                    q = (b - 2) % B
                    wait_if_positive(act, max_ready, 1, i, b - 1)
                    wait_if_positive(act, probT_psum, 1, i, b - 3)
                    for t in range(T):
                        nc.scalar.activation(prob[:, b % 2, t, :], logits[:, b % 2, t, :], ACT.Exp,
                                             bias=neg_max[:, q, t:t + 1],
                                             accum_out=prob_sum[:, q, t:t + 1]).then_inc(prob_ready, 1)
                if live(3):
                    square(b, i, 1)
                if live(0):
                    hi_part(b, i, 1)
                if live(2):
                    wait_if_positive(act, probT_psum, 1, i, b - 1)
                    wait_if_positive(act, mix_psum, T, i, T * (b - 4) + T)
                    nc.scalar.activation(prob_hi[:, b % 2, :], psE[0:S, 0:T * P], ACT.Copy).then_inc(prob_hi_ready, 1)
                if live(3):
                    q = (b - 3) % B
                    wait_if_positive(act, shift2_ready, 1, i, b - 2)
                    stored = i + (b - 3) // B
                    if not isinstance(stored, int) or stored > 0:
                        act.wait_ge(out_stored[q], 16 * stored)
                    for t in range(T):
                        nc.scalar.activation(zs[:, q, t, :], hid[:, (b - 3) % 2, t, :], ACT.Identity,
                                             bias=shift2[:, q, t:t + 1], scale=rstd2[:, q, t:t + 1]).then_inc(z_ready, 1)

            for t in range(T):
                hi_part(0, 0, t)
            value_hi(3)
            pipeline(act, body)

        @block.vector
        def _(dve):
            own = [0]

            def link(ins):
                own[0] += 1
                ins.then_inc(dve_own, 1)
                dve.wait_ge(dve_own, own[0])

            for n in range(2):
                k = 2 * n
                dve.wait_ge(wt_loaded[n], 16)
                link(nc.vector.reduce_sum(sums[:, 8 + k:9 + k], wt[:, k, :], axis=AX_X))
                link(nc.vector.tensor_scalar(sums[:, k:k + 1], sums[:, 8 + k:9 + k], -1.0 / H, None, ALU.mult))
                nc.vector.tensor_scalar(wt[:, k, :], wt[:, k, :], sums[:, k:k + 1], None, ALU.add).then_inc(wc_ready, 1)
                dve.wait_ge(act_own, n + 2)
                nc.vector.tensor_scalar(wt[:, k + 1, :], wt[:, k + 1, :], sums[:, k + 1:k + 2], None, ALU.add).then_inc(wc_ready, 1)
            dve.wait_ge(vec_psum, 1)
            nc.vector.tensor_copy(vec_cols[:], psE[:, 0:4 * KH]).then_inc(vec_ready, 1)
            dve.wait_ge(vec_ready, 1)
            nc.vector.tensor_scalar(g1s[:], vec_cols[:, 0:KH], SCALE, None, ALU.mult).then_inc(g1s_ready, 1)
            for k in range(KH):
                dve.wait_ge(wtT_hi_ready, k + 1)
                nc.vector.tensor_tensor(wtT_lo[:, k, :], W_BANK[k], f32(wtT_hi[:, k, :]), ALU.subtract).then_inc(wtT_lo_ready, 1)
            dve.wait_ge(bt_loaded, 16)
            link(nc.vector.reduce_sum(sums[:, 4:5], bt_rows[:], axis=AX_X))
            link(nc.vector.tensor_scalar(sums[:, 5:6], sums[:, 4:5], -1.0 / H, None, ALU.mult))
            nc.vector.tensor_scalar(bt_rows[:], bt_rows[:], sums[:, 5:6], None, ALU.add).then_inc(bc_ready, 1)
            dve.wait_ge(bc_ready, 1)
            dve.wait_ge(wc_ready, KD)
            for k in range(KD):
                nc.vector.tensor_tensor_reduce(out=waste_dve[:, k, :], in0=wt[:, k, :], in1=bt_rows[:], scale=2.0 / H, scalar=0.0,
                                               op0=ALU.mult, op1=ALU.add, accum_out=lin[:, k:k + 1]).then_inc(lin_ready, 1)
            for k in range(KH):
                dve.wait_ge(vT_ready, k + 1)
                nc.vector.tensor_copy(vT_hi[:, k, :], vT[:, k, :]).then_inc(vT_hi_ready, 1)
            dve.wait_ge(lin_ready, KD)
            nc.vector.tensor_tensor_reduce(out=waste_dve[:, 0, :], in0=bt_rows[:], in1=bt_rows[:], scale=1.0 / H, scalar=EPS,
                                           op0=ALU.mult, op1=ALU.add, accum_out=sums[:, 6:7]).then_inc(dve_own, 1)
            own[0] += 1
            dve.wait_ge(extras_ready, 1 + KD)
            for k in range(KD):
                at = SCORE_AT[k] + LIN
                nc.vector.tensor_copy(proj_hi[:, :, at], lin[:, k:k + 1].to_broadcast([P, B])).then_inc(lin_hi_ready, 1)
            dve.wait_ge(dve_own, own[0])
            nc.vector.tensor_copy(score_c[:, :, LIN], sums[:, 6:7].to_broadcast([P, B]))
            dve.wait_ge(lin_hi_ready, KD)
            for k in range(KD):
                at = SCORE_AT[k] + LIN
                nc.vector.tensor_tensor(proj_lo[:, :, at], lin[:, k:k + 1].to_broadcast([P, B]),
                                        f32(proj_hi[:, :, at]), ALU.subtract).then_inc(lin_lo_ready, 1)

            def t_lo(parts):
                for part, (k, at, n) in parts:
                    dve.wait_ge(g_hi, max(part + 1, 2))
                    if k == 0:
                        skip = 0 if at == DIAG0 else P
                        nc.vector.scalar_tensor_tensor(proj_lo[:, 0, at:at + n], W_BANK[k][:, skip:skip + n],
                                                       (1.0 if at == DIAG0 else 2.0) / H, f32(proj_hi[:, 0, at:at + n]),
                                                       ALU.mult, ALU.subtract).then_inc(g_lo, 1)
                    else:
                        last = nc.vector.scalar_tensor_tensor(proj_lo[:, 0, at:at + P], W_BANK[k][:, 0:P], 1.0 / H,
                                                              f32(proj_hi[:, 0, at:at + P]), ALU.mult, ALU.subtract)
                        if n > P:
                            last = nc.vector.scalar_tensor_tensor(proj_lo[:, 0, at + P:at + n], W_BANK[k][:, P:n], 2.0 / H,
                                                                  f32(proj_hi[:, 0, at + P:at + n]), ALU.mult, ALU.subtract)
                        last.then_inc(g_lo, 1)

            t_lo(list(enumerate(T_PARTS))[0:2])
            dve.wait_ge(mean_psum, 1)
            for k in range(KH):
                nc.vector.tensor_tensor(kT[:, k, :], vT[:, k, :], psA[:, 0, 0:BS], ALU.subtract).then_inc(kc_ready, 1)
            for k in range(1, KH):
                dve.wait_ge(ksq_ready, k + 1)
                if k > 1:
                    dve.wait_ge(ksqsum_ready, k - 1)
                nc.vector.tensor_tensor(kSqSum, kSq[:, 0, :] if k == 1 else kSqSum, kSq[:, k, :], ALU.add).then_inc(ksqsum_ready, 1)
            link(nc.vector.memset(kvar[:], 1.0))
            dve.wait_ge(osums_ready, 1)
            for k in range(KH):
                nc.vector.tensor_scalar(wo_hi[:, k, :], wo[:, k, :], osums[:, k:k + 1], None, ALU.add).then_inc(wo_hi_ready, 1)
                if k == 1:
                    dve.wait_ge(kvar_psum, 1)
                    for n, (at, w) in enumerate(KEYS):
                        last = nc.vector.tensor_scalar(kvar[0:w, n:n + 1], psA[0:w, 1, n:n + 1], EPS, None, ALU.add)
                    last.then_inc(kvar_ready, 1)
                if k >= 1:
                    dve.wait_ge(wo_hi_ready, k)
                    nc.vector.scalar_tensor_tensor(wo_lo[:, k - 1, :], wo[:, k - 1, :], osums[:, k - 1:k], f32(wo_hi[:, k - 1, :]),
                                                   ALU.add, ALU.subtract).then_inc(wo_ready, 1)
            dve.wait_ge(wo_hi_ready, KH)
            nc.vector.scalar_tensor_tensor(wo_lo[:, KH - 1, :], wo[:, KH - 1, :], osums[:, KH - 1:KH], f32(wo_hi[:, KH - 1, :]),
                                           ALU.add, ALU.subtract).then_inc(wo_ready, 1)
            dve.wait_ge(krstd_ready, 1)
            for n, (at, w) in enumerate(KEYS):
                last = nc.vector.tensor_scalar(diag[0:w, at:at + w], ident[0:w, 0:w], krstd[0:w, n:n + 1], None, ALU.mult)
            last.then_inc(diag_ready, 1)
            t_lo(list(enumerate(T_PARTS))[2:])
            dve.wait_ge(btT_hi_ready, 1)
            nc.vector.tensor_tensor(btT_lo[:], psB[:].rearrange("p (k m) -> p k m", k=KH), f32(btT_hi[:]), ALU.subtract).then_inc(rowsT_ready, 1)
            dve.wait_ge(krows_psum, 1)
            for k in range(KH):
                nc.vector.scalar_tensor_tensor(kT[:, k, :], kT[:, k, :], vec_cols[:, KH + k:KH + k + 1], psA[:, 0, 0:BS],
                                               ALU.mult, ALU.mult).then_inc(kn_ready, 1)

            def value(b):
                dve.wait_ge(val_psum, b + 1)
                nc.vector.tensor_tensor(vbuf[:, b, :], VAL_BANK[b][0:S, :], bo_rows[0:S, :], ALU.add).then_inc(val_ready, 1)

            def value_lo(b):
                dve.wait_ge(val_hi_ready, b + 1)
                nc.vector.tensor_tensor(val_lo[:, b, :], vbuf[:, b, :], f32(val_hi[:, b, :]), ALU.subtract).then_inc(val_lo_ready, 1)

            dve.wait_ge(bo_ready, 1)
            value(0)
            for k in range(KH):
                dve.wait_ge(kg_hi_ready, k + 1)
                nc.vector.scalar_tensor_tensor(kg_lo[:, k, :], kT[:, k, :], g1s[:, k:k + 1], f32(kg_hi[:, k, :]),
                                               ALU.mult, ALU.subtract).then_inc(kg_lo_ready, 1)
            value(1)
            value(2)
            dve.wait_ge(cd_psum, 1)
            nc.vector.tensor_copy(score_d[:], psA[:, 1, 0:BS].rearrange("p (b s) -> p b s", b=B)).then_inc(cd_ready, 1)
            dve.wait_ge(cd_psum, 2)
            nc.vector.tensor_copy(score_c[:, :, 0:S], psA[:, 0, 0:BS].rearrange("p (b s) -> p b s", b=B)).then_inc(cd_ready, 1)
            for b in range(3):
                value_lo(b)
            for k in range(KD):
                dve.wait_ge(m_hi, k + 1)
                dst = slice(SCORE_AT[k], SCORE_AT[k] + S)
                nc.vector.tensor_tensor(proj_lo[:, :, dst], M_BANK[k][:, 0:BS].rearrange("p (b s) -> p b s", b=B),
                                        f32(proj_hi[:, :, dst]), ALU.subtract).then_inc(m_lo, 1)

            def lo_part(b, i, t):
                wait_if_positive(dve, x_hi_ready, T, i, T * b + t + 1)
                nc.vector.tensor_tensor(x_lo[:, b % 2, t, :], psT[:, t, :], f32(x_hi[:, b % 2, t, :]),
                                        ALU.subtract).then_inc(x_lo_ready, 1)

            def quadratic(b, i, t, lag):
                q = (b - lag) % B
                wait_if_positive(dve, proj_psum, T, i, T * (b - lag) + t + 1)
                nc.vector.tensor_tensor(sc[:, q, t, :], psA[:, t, YW:YW + SW], score_c[:, q, :], ALU.add).then_inc(sc_ready, 1)
                wait_if_positive(dve, quad_ready, T, i, T * (b - lag - 1) + t + 1)
                nc.vector.tensor_tensor_reduce(out=waste_dve[:, 2 * t, 0:YW], in0=psA[:, t, 0:YW], in1=xs[:, q, t, P:D],
                                               scale=1.0, scalar=0.0, op0=ALU.mult, op1=ALU.add,
                                               accum_out=quad_a[:, q, t:t + 1])
                wait_if_positive(dve, sc_ready, T, i, T * (b - lag) + t + 1)
                nc.vector.tensor_tensor_reduce(out=waste_dve[:, 2 * t + 1, 0:P], in0=psB[:, 0:P], in1=xs[:, q, t, 0:P],
                                               scale=1.0, scalar=sc[:, q, t, LIN:LIN + 1], op0=ALU.mult, op1=ALU.add,
                                               accum_out=quad_b[:, q, t:t + 1]).then_inc(quad_ready, 1)

            def residual(b, i, t):
                q = (b - 3) % B
                wait_if_positive(dve, mix_psum, T, i, T * (b - 3) + t + 1)
                wait_if_positive(dve, inv_ready, 1, i, b - 2)
                nc.vector.scalar_tensor_tensor(hid[:, (b - 3) % 2, t, :], psO[:, t, :], inv_sum[:, q, t:t + 1],
                                               xs[:, q, t, :], ALU.mult, ALU.add).then_inc(hid_ready, 1)

            def body(b, i, live):
                if live(2):
                    q = (b - 2) % B
                    quadratic(b, i, 1, 2)
                    wait_if_positive(dve, quad_ready, T, i, T * (b - 2) + T)
                    nc.vector.tensor_tensor(var[:, q, :], quad_a[:, q, :], quad_b[:, q, :], ALU.add).then_inc(var_sum, 1)
                if live(3):
                    residual(b, i, 0)
                if live(2):
                    wait_if_positive(dve, var_sum, 1, i, b - 1)
                    nc.vector.tensor_scalar(var[:, q, :], var[:, q, :], EPS, None, ALU.max).then_inc(var_ready, 1)
                if live(0):
                    lo_part(b, i, 0)
                if live(2):
                    wait_if_positive(dve, rstd_ready, 1, i, b - 1)
                    wait_if_positive(dve, prob_ready, T, i, T * (b - 4) + T)
                    for t in range(T):
                        nc.vector.scalar_tensor_tensor(logits[:, b % 2, t, :], sc[:, q, t, 0:S], rstd[:, q, t:t + 1],
                                                       score_d[:, q, :], ALU.mult, ALU.add).then_inc(logits_ready, 1)
                    wait_if_positive(dve, logits_ready, T, i, T * (b - 2) + T)
                    nc.vector.reduce_max(neg_max[:, q, :], logits[:, b % 2, :, :], axis=AX_X, negate=True).then_inc(max_ready, 1)
                if live(3):
                    residual(b, i, 1)
                if live(2):
                    wait_if_positive(dve, prob_ready, T, i, T * (b - 2) + T)
                    nc.vector.reciprocal(inv_sum[:, q, :], prob_sum[:, q, :]).then_inc(inv_ready, 1)
                if live(1):
                    quadratic(b, i, 0, 1)
                if live(2):
                    wait_if_positive(dve, prob_hi_ready, 1, i, b - 1)
                    nc.vector.tensor_tensor(prob_lo[:, b % 2, :], psE[0:S, 0:T * P], f32(prob_hi[:, b % 2, :]),
                                            ALU.subtract).then_inc(prob_lo_ready, 1)
                if live(0):
                    lo_part(b, i, 1)

            lo_part(0, 0, 0)
            value(3)
            lo_part(0, 0, 1)
            value_lo(3)
            dve.wait_ge(cd_ready, 2)
            pipeline(dve, body)

        @block.tensor
        def _(pe):
            def parts3(a_hi, a_lo, b_hi, b_lo):
                return (a_hi, b_hi), (a_hi, b_lo), (a_lo, b_hi)

            pe.wait_ge(ident_ready, 1)
            pe.wait_ge(ctx_loaded, 16)
            for k in range(KA):
                for b in range(B):
                    last = nc.tensor.transpose(V_BANK[k][:, b * S:(b + 1) * S], cx[:, b, k * P:(k + 1) * P], ident[0:S, 0:S])
                last.then_inc(cxT_psum, 1)
            for j in range(KD):
                pe.wait_ge(wc_ready, j + 1)
                for k in range(KH):
                    last = nc.tensor.transpose(W_BANK[k][:, j * P:(j + 1) * P], wt[:, j, k * P:(k + 1) * P], ident[:])
                    if j == KD - 1:
                        last.then_inc(wtT_psum, 1)
            pe.wait_ge(vec_loaded, 64)
            nc.tensor.transpose(psE[:, 0:4 * KH], vec_rows[:], ident[0:4 * KH, 0:4 * KH]).then_inc(vec_psum, 1)
            pe.wait_ge(wa_loaded, 16)
            pe.wait_ge(cxT_ready, KA)
            for k in range(KH):
                if k == KH - 1:
                    pe.wait_ge(vec_ready, 1)
                for j in range(KA):
                    last = nc.tensor.matmul(V_BANK[k][:, 0:BS], wa[:, j, k * P:(k + 1) * P], cxT[:, j, :],
                                            start=(j == 0), stop=(j == KA - 1))
                last.then_inc(vT_psum, 1)

            def gram(k):
                passes = [(h, a, w) for h in range(KH) for a, w in parts3(wtT_hi, wtT_lo, wtT_hi, wtT_lo)]
                for n, (h, a, w) in enumerate(passes):
                    last = nc.tensor.matmul(W_BANK[k][:, 0:D - k * P], a[:, h, k * P:(k + 1) * P], w[:, h, k * P:D],
                                            start=(n == 0), stop=(n == len(passes) - 1))
                last.then_inc(g_psum, 1)

            pe.wait_ge(wtT_lo_ready, KH)
            gram(0)
            pe.wait_ge(ones_ready, 2)
            pe.wait_ge(vT_ready, KH)
            for k in range(KH):
                last = nc.tensor.matmul(psA[:, 0, 0:BS], mean_of, vT[:, k, :], start=(k == 0), stop=(k == KH - 1))
            last.then_inc(mean_psum, 1)
            for k in range(1, KD):
                gram(k)
            pe.wait_ge(ksqsum_ready, KH - 1)
            for n, (at, w) in enumerate(KEYS):
                last = nc.tensor.matmul(psA[0:w, 1, n:n + 1], kSqSum[:, at:at + w], mean_of[:, 0:1], start=True, stop=True)
            last.then_inc(kvar_psum, 1)
            pe.wait_ge(bc_ready, 1)
            for k in range(KH):
                last = nc.tensor.transpose(psB[:, k * P:(k + 1) * P], bt_rows[:, k * P:(k + 1) * P], ident[:])
            last.then_inc(rowsT_psum, 1)
            pe.wait_ge(beta1_loaded, 16)
            for k in range(KH):
                last = nc.tensor.transpose(psE[:, k * P:(k + 1) * P], beta1_rows[:, k * P:(k + 1) * P], ident[:])
            last.then_inc(rowsT_psum, 1)

            def values_product(b):
                if b == 2:
                    pe.wait_ge(val_ready, 1)
                passes = [(h, a, w) for h in range(KH) for a, w in parts3(vT_hi, vT_lo, wo_hi, wo_lo)]
                for n, (h, a, w) in enumerate(passes):
                    last = nc.tensor.matmul(VAL_BANK[b][0:S, :], a[:, h, b * S:(b + 1) * S], w[:, h, :],
                                            start=(n == 0), stop=(n == len(passes) - 1))
                last.then_inc(val_psum, 1)

            pe.wait_ge(diag_ready, 1)
            for at, w in KEYS:
                last = nc.tensor.matmul(psA[:, 0, at:at + w], ones[0:w, :], diag[0:w, at:at + w], start=True, stop=True)
            last.then_inc(krows_psum, 1)
            pe.wait_ge(wo_ready, KH)
            pe.wait_ge(vT_lo_ready, KH)
            pe.wait_ge(rowsT_ready, 2)
            for b in range(3):
                values_product(b)
            pe.wait_ge(kT_ready, KH)
            for h in range(KH):
                last = nc.tensor.matmul(psA[:, 1, 0:BS], beta1T[:, h, :], kT[:, h, :], start=(h == 0), stop=(h == KH - 1))
            last.then_inc(cd_psum, 1)
            pe.wait_ge(kg_lo_ready, KH)
            passes = [(h, a, w) for h in range(KH) for a, w in parts3(btT_hi, btT_lo, kg_hi, kg_lo)]
            for n, (h, a, w) in enumerate(passes):
                last = nc.tensor.matmul(psA[:, 0, 0:BS], a[:, h, :], w[:, h, :], start=(n == 0), stop=(n == len(passes) - 1))
            last.then_inc(cd_psum, 1)
            passes = [(h, a, w) for h in range(KH) for a, w in parts3(wtT_hi, wtT_lo, kg_hi, kg_lo)]
            for k in range(KD):
                pe.wait_ge(g_lo, len(T_PARTS))
                pe.wait_ge(val_ready, 3)
                for n, (h, a, w) in enumerate(passes):
                    last = nc.tensor.matmul(M_BANK[k][:, 0:BS], a[:, h, k * P:(k + 1) * P], w[:, h, :],
                                            start=(n == 0), stop=(n == len(passes) - 1))
                last.then_inc(m_psum, 1)

            def transpose_x(b, i, t):
                pe.wait_ge(x_loaded[b][t], 16 * (i + 1))
                wait_if_positive(pe, x_lo_ready, T, i, T * (b - 1) + t + 1)
                for k in range(KD):
                    last = nc.tensor.transpose(psT[:, t, k * P:(k + 1) * P], xs[:, b, t, k * P:(k + 1) * P], ident[:])
                last.then_inc(xT_psum, 1)

            pe.wait_ge(g_lo, len(T_PARTS))
            for t in range(T):
                transpose_x(0, 0, t)
            pe.wait_ge(cd_ready, 2)
            values_product(3)
            pe.wait_ge(m_lo, KD)
            pe.wait_ge(lin_lo_ready, KD)

            PASSES = [(a, w, k) for k in range(KD) for a, w in ((x_hi, proj_hi), (x_hi, proj_lo), (x_lo, proj_hi))]

            def project(b, i, t, first, count):
                q, par = (b - 1) % B, (b - 1) % 2
                if isinstance(i, int) and (i, b, t, first) == (0, 2, 0, 0):
                    pe.wait_ge(t_copied, 2 * 16 * len(T_PARTS))
                if first == 0:
                    wait_if_positive(pe, x_lo_ready, T, i, T * (b - 1) + t + 1)
                    wait_if_positive(pe, quad_ready, T, i, T * (b - 2) + t + 1)
                for n in range(first, first + count):
                    part, w, k = PASSES[n]
                    skip = 0 if k == 0 else (k - 1) * P
                    nc.tensor.matmul(psA[:, t, skip:YW + SW], part[:, par, t, k * P:(k + 1) * P],
                                     w[:, q, OFFSET[k]:OFFSET[k] + WIDTH[k]], start=(n == 0), stop=(n == len(PASSES) - 1))

            def project_diagonal(b, i, t):
                q, par = (b - 1) % B, (b - 1) % 2
                wait_if_positive(pe, quad_ready, T, i, T * (b - 1) + t)
                for n in range(3):
                    part, w, _ = PASSES[n]
                    last = nc.tensor.matmul(psB[:, 0:P], part[:, par, t, 0:P], w[:, q, DIAG0:DIAG0 + P],
                                            start=(n == 0), stop=(n == 2))
                last.then_inc(proj_psum, 1)

            def body(b, i, live):
                half = len(PASSES) // 3
                if live(0):
                    transpose_x(b, i, 0)
                if live(1):
                    project(b, i, 0, 0, len(PASSES))
                    project_diagonal(b, i, 0)
                if live(0):
                    transpose_x(b, i, 1)
                if live(1):
                    project(b, i, 1, 0, half)
                if live(2):
                    wait_if_positive(pe, prob_ready, T, i, T * (b - 2) + T)
                    wait_if_positive(pe, prob_lo_ready, 1, i, b - 2)
                    for t in range(T):
                        last = nc.tensor.transpose(psE[0:S, t * P:(t + 1) * P], prob[:, b % 2, t, :], ident[:])
                    last.then_inc(probT_psum, 1)
                if live(1):
                    project(b, i, 1, half, len(PASSES) - half)
                    project_diagonal(b, i, 1)
                if live(2):
                    q = (b - 2) % B
                    wait_if_positive(pe, prob_lo_ready, 1, i, b - 1)
                    if isinstance(i, int) and (i, b) == (0, 2):
                        pe.wait_ge(val_lo_ready, B)
                    for t in range(T):
                        wait_if_positive(pe, hid_ready, T, i, T * (b - 3) + t + 1)
                        for n, (pr, v) in enumerate(((prob_hi, val_hi), (prob_hi, val_lo), (prob_lo, val_hi))):
                            last = nc.tensor.matmul(psO[:, t, :], pr[:, b % 2, t * P:(t + 1) * P], v[:, q, :],
                                                    start=(n == 0), stop=(n == 2))
                        last.then_inc(mix_psum, 1)

            pipeline(pe, body)


_PRE = "L0_xattn_"
_INS = ["x", "ctx_768"] + [_PRE + n for n in ("W_text", "b_text", "W_audio", "b_audio", "W_out", "b_out",
                                              "g1", "beta1", "g2", "beta2", "g_out", "beta_out")]


def kernel(**inputs):
    import numpy as _np
    import concourse.bacc as _bacc
    from concourse import mybir as _mybir
    from concourse.bass_utils import run_bass_kernel_spmd as _run

    nc = _bacc.Bacc("TRN2", target_bir_lowering=False, num_devices=1)
    arrays, args = {}, []
    for name in _INS:
        a = _np.ascontiguousarray(inputs[name])
        arrays[f"in_{name}_dram"] = a
        args.append(nc.dram_tensor(f"in_{name}_dram", a.shape, _mybir.dt.from_np(a.dtype), kind="ExternalInput").ap())
    shape = inputs["x"].shape
    args.append(nc.dram_tensor("out_dram", shape, _mybir.dt.float32, kind="ExternalOutput").ap())
    cross_attention(nc, *args)
    r = _run(nc, [arrays], core_ids=[0])
    return r.results[0]["out_dram"]
```

```python
from contextlib import ExitStack

import concourse.bass as bass
from concourse import mybir

F32 = mybir.dt.float32
F32R = mybir.dt.float32r
ALU = mybir.AluOpType
ACT = mybir.ActivationFunctionType
AX_X = mybir.AxisListType.X

P = 128
EPS = 1e-5


def cross_attention(nc, x, ctx, w_text, b_text, w_audio, b_audio, w_out, b_out,
                    g1, beta1, g2, beta2, g_out, beta_out, out):
    B, L, D = x.shape
    _, S, DA = ctx.shape
    H = w_text.shape[1]
    KD, KA, KH = D // P, DA // P, H // P
    SCALE = float(H) ** -0.5
    assert D == H == 4 * P and DA % P == 0 and S < P

    T = 2
    ROWS = T * P
    STEPS = B * L // ROWS
    PER_BATCH = L // ROWS
    BS = B * S
    KEYS = [(at, min(P, BS - at)) for at in range(0, BS, P)]
    SW = S + 3
    LIN, NXBAR = S, S + 1
    YW = D - P
    YB = 2 * P - SW
    WIDTH = [D - YB] + [D - k * P + SW for k in range(1, KD)]
    SKIP = [YB - P] + [(k - 1) * P for k in range(1, KD)]
    OFFSET = [0] + [D + SW + sum(WIDTH[1:k]) for k in range(1, KD)]
    BANK_B = WIDTH[0]
    COLS = D + SW + sum(WIDTH[1:])
    SCORE_AT = [D] + [OFFSET[k] + WIDTH[k] - SW for k in range(1, KD)]

    with ExitStack() as stack:
        def sb(name, shape, dt=F32):
            return stack.enter_context(nc.sbuf_tensor(name, shape, dt))

        def sem(name):
            return stack.enter_context(nc.semaphore(name))

        psT = stack.enter_context(nc.psum_tensor("psT", [P, T, 512], F32))
        psA = stack.enter_context(nc.psum_tensor("psA", [P, T, 512], F32))
        psB = stack.enter_context(nc.psum_tensor("psB", [P, 512], F32))
        psE = stack.enter_context(nc.psum_tensor("psE", [P, 512], F32))
        psO = stack.enter_context(nc.psum_tensor("psO", [P, T, 512], F32))

        ident = sb("ident", [P, P])
        proj_hi = sb("proj_hi", [P, B, COLS], F32R)
        proj_lo = sb("proj_lo", [P, B, COLS], F32R)
        val_hi = sb("val_hi", [S, B, H], F32R)
        val_lo = sb("val_lo", [S, B, H], F32R)
        score_c = sb("score_c", [P, B, SW])
        score_d = sb("score_d", [P, B, S])
        gain = sb("gain", [P, H])
        shift = sb("shift", [P, H])
        neg_half = sb("neg_half", [P, 4])
        xs = sb("xs", [P, B, T, D])
        x_hi = sb("x_hi", [P, 2, T, D], F32R)
        x_lo = sb("x_lo", [P, 2, T, D], F32R)
        sc = sb("sc", [P, B, T, SW])
        sc_part = sb("sc_part", [P, T, SW])
        quad_a = sb("quad_a", [P, B, T])
        quad_b = sb("quad_b", [P, B, T])
        var = sb("var", [P, B, T])
        rstd = sb("rstd", [P, B, T])
        logits = sb("logits", [P, 2, T, S])
        neg_max = sb("neg_max", [P, B, T])
        prob = sb("prob", [P, 2, T, S])
        prob_sum = sb("prob_sum", [P, B, T])
        inv_sum = sb("inv_sum", [P, B, T])
        prob_hi = sb("prob_hi", [S, 2, T * P], F32R)
        prob_lo = sb("prob_lo", [S, 2, T * P], F32R)
        hid = sb("hid", [P, 2, T, H])
        sq_sum = sb("sq_sum", [P, B, T])
        var2 = sb("var2", [P, B, T])
        rstd2 = sb("rstd2", [P, B, T])
        shift2 = sb("shift2", [P, B, T])
        zs = sb("zs", [P, B, T, H])
        waste_dve = sb("waste_dve", [P, 4, H], mybir.dt.bfloat16)
        waste_act = sb("waste_act", [P, 2, H], mybir.dt.bfloat16)

        VECS = (g1, g2, beta2, b_audio, beta1, b_text)
        vec_rows = sb("vec_rows", [len(VECS) * KH, P])
        vec_cols = sb("vec_cols", [P, len(VECS) * KH])
        g1s = sb("g1s", [P, KH])
        bt_rows = sb("bt_rows", [P, H])
        bo_rows = sb("bo_rows", [P, H])
        cd_cols = sb("cd_cols", [P, KH, 2])
        cd_rows = sb("cd_rows", [2, BS])
        pick = sb("pick", [2, 2, P])
        sums = sb("sums", [P, 16])
        osums = sb("osums", [P, KH + 1])
        lin = sb("lin", [P, KD])
        wa = sb("wa", [P, KA, H])
        cxT = sb("cxT", [P, KA, BS])
        vT = sb("vT", [P, KH, BS])
        vT_hi = sb("vT_hi", [P, KH, BS], F32R)
        vT_lo = sb("vT_lo", [P, KH, BS], F32R)
        kg_hi = sb("kg_hi", [P, KH, BS], F32R)
        kg_lo = sb("kg_lo", [P, KH, BS], F32R)
        wo_hi = sb("wo_hi", [P, KH, H], F32R)
        wo_lo = sb("wo_lo", [P, KH, H], F32R)
        kvar = sb("kvar", [P, 4])
        krstd = sb("krstd", [P, 4])
        room = [zs[:].rearrange("p b t h -> p (b t h)"), hid[:].rearrange("p c t h -> p (c t h)")]
        used = [0, 0]

        def borrow(where, n):
            used[where] += n
            assert used[where] <= room[where].shape[1]
            return room[where][:, used[where] - n:used[where]]

        values = borrow(0, B * H)
        vbuf = values[:, 0:len(KEYS) * H].rearrange("p (n h) -> p n h", n=len(KEYS))
        cx = values[:, 0:B * DA].rearrange("p (b d) -> p b d", b=B)[0:S]
        kSq = borrow(0, KH * BS).rearrange("p (k n) -> p k n", k=KH)
        kSqSum = borrow(0, BS)
        kT = borrow(1, KH * BS).rearrange("p (k n) -> p k n", k=KH)
        mean_of = borrow(1, P)
        mean_r = kg_hi[:, 0, 0:P]
        ones = borrow(1, P)
        diag = borrow(1, BS)
        assert len(KEYS) <= KA
        vb_hi = wa[:, 0:len(KEYS), :].bitcast(F32R)
        wt = xs[:, 0:2].rearrange("p b t d -> p (b t) d")
        wo = xs[:, 2:4].rearrange("p b t d -> p (b t) d")
        wtT_hi = x_hi[:].rearrange("p c t d -> p (c t) d")
        wtT_lo = x_lo[:].rearrange("p c t d -> p (c t) d")

        wt_loaded = [sem(f"wt_loaded{k}") for k in range(KD)]
        wa_loaded, wo_loaded = sem("wa_loaded"), sem("wo_loaded")
        ctx_loaded, vec_loaded = sem("ctx_loaded"), sem("vec_loaded")
        bt_loaded, bo_loaded = sem("bt_loaded"), sem("bo_loaded")
        gs_loaded, t_copied = sem("gs_loaded"), sem("t_copied")
        mean_r_ready = sem("mean_r_ready")
        ident_ready, ones_ready, gain_ready = sem("ident_ready"), sem("ones_ready"), sem("gain_ready")
        cxT_psum, cxT_ready = sem("cxT_psum"), sem("cxT_ready")
        vec_psum, vec_ready = sem("vec_psum"), sem("vec_ready")
        g1s_ready = sem("g1s_ready")
        vT_psum, vT_ready, vT_hi_ready, vT_lo_ready = sem("vT_psum"), sem("vT_ready"), sem("vT_hi_ready"), sem("vT_lo_ready")
        wc_ready, wtT_psum = sem("wc_ready"), sem("wtT_psum")
        wtT_hi_ready, wtT_lo_ready, lin_ready = sem("wtT_hi_ready"), sem("wtT_lo_ready"), sem("lin_ready")
        bc_ready, cd_cols_ready, pick_ready = sem("bc_ready"), sem("cd_cols_ready"), sem("pick_ready")
        cd_rows_psum, cd_rows_ready = sem("cd_rows_psum"), sem("cd_rows_ready")
        g_psum, g_hi, g_lo = sem("g_psum"), sem("g_hi"), sem("g_lo")
        mean_psum, kc_ready, ksq_ready, kvar_psum = sem("mean_psum"), sem("kc_ready"), sem("ksq_ready"), sem("kvar_psum")
        ksqsum_ready, diag_ready, krows_psum = sem("ksqsum_ready"), sem("diag_ready"), sem("krows_psum")
        kvar_ready, krstd_ready, kn_ready, kT_ready = sem("kvar_ready"), sem("krstd_ready"), sem("kn_ready"), sem("kT_ready")
        kg_hi_ready, kg_lo_ready = sem("kg_hi_ready"), sem("kg_lo_ready")
        osums_ready, wo_centred, wo_hi_ready = sem("osums_ready"), sem("wo_centred"), sem("wo_hi_ready")
        wo_ready, bo_ready, val_placed = sem("wo_ready"), sem("bo_ready"), sem("val_placed")
        val_psum, val_ready, val_hi_ready, val_lo_ready = sem("val_psum"), sem("val_ready"), sem("val_hi_ready"), sem("val_lo_ready")
        m_psum, m_hi, m_lo, cd_psum, cd_ready = sem("m_psum"), sem("m_hi"), sem("m_lo"), sem("cd_psum"), sem("cd_ready")
        extras_ready, lin_hi_ready, lin_lo_ready = sem("extras_ready"), sem("lin_hi_ready"), sem("lin_lo_ready")
        dve_own, pool_own, act_own = sem("dve_own"), sem("pool_own"), sem("act_own")

        W_BANK = (psT[:, 0], psT[:, 1], psO[:, 0], psO[:, 1])
        V_BANK = (psA[:, 0], psA[:, 1], psB[:], psE[:])
        VAL_BANK = (psT[:, 0], psT[:, 1], psA[:, 1])
        M_BANK = (psO[:, 0], psO[:, 1], psA[:, 0], psA[:, 1])
        C_BANK, D_BANK = psE[:], psO[:, 0]
        T_PIECES = [[(BANK_B, P, 0), (BANK_B + P, YB - P, P), (0, D - YB, YB)]]
        T_PIECES += [[(OFFSET[k], P, 0)] + ([(OFFSET[k] + P, D - (k + 1) * P, P)] if k < KD - 1 else []) for k in range(1, KD)]

        x_loaded = [[sem(f"x_loaded{b}{t}") for t in range(T)] for b in range(B)]
        out_stored = [sem(f"out_stored{b}") for b in range(B)]
        xT_psum, x_hi_ready, x_lo_ready = sem("xT_psum"), sem("x_hi_ready"), sem("x_lo_ready")
        projB_psum, proj_psum = sem("projB_psum"), sem("proj_psum")
        part_ready, sc_ready, quadB_ready, quad_ready = sem("part_ready"), sem("sc_ready"), sem("quadB_ready"), sem("quad_ready")
        var_ready = sem("var_ready")
        rstd_ready = sem("rstd_ready")
        logits_ready = sem("logits_ready")
        max_ready = sem("max_ready")
        prob_ready = sem("prob_ready")
        inv_ready, probT_psum = sem("inv_ready"), sem("probT_psum")
        prob_hi_ready, prob_lo_ready = sem("prob_hi_ready"), sem("prob_lo_ready")
        mix_psum, hid_ready, sq_ready = sem("mix_psum"), sem("hid_ready"), sem("sq_ready")
        var2_ready, rstd2_ready, shift2_ready = sem("var2_ready"), sem("rstd2_ready"), sem("shift2_ready")
        z_ready, zg_ready, out_ready = sem("z_ready"), sem("zg_ready"), sem("out_ready")
        SHARED = STEPS - 3
        zg_tail, out_tail = sem("zg_tail"), sem("out_tail")

        SEGMENTS = sum(1 for at, w in KEYS for q in range(B) if max(q * S, at) < min((q + 1) * S, at + w))
        f32 = lambda ap: ap.bitcast(F32)

        def pipeline(eng, body):
            for b in range(1, B):
                body(b, 0, lambda lag, b=b: b - lag >= 0)
            with eng.Fori(1, STEPS // B) as i:
                for b in range(B):
                    body(b, i, lambda lag: True)
            for b in range(B):
                body(b, STEPS // B, lambda lag, b=b: b - lag < 0)

        assert T == 2 and B == 4

        def tail(i, b):
            return isinstance(i, int) and (i, b) in ((STEPS // B, 1), (STEPS // B, 2), (STEPS // B, 3))

        def wait_if_positive(eng, s, per, i, const):
            value = per * B * i + const
            if isinstance(i, int) and value <= 0:
                return
            eng.wait_ge(s, value)

        block = stack.enter_context(nc.Block())

        @block.sync
        def _(sp):
            wt_rows = w_text.rearrange("(k p) h -> p k h", p=P)
            for k in range(KD):
                sp.dma_start(wt[:, k, :], wt_rows[:, k, :]).then_inc(wt_loaded[k], 16)
                if k == 1:
                    sp.dma_start(cx, ctx.rearrange("b s d -> s b d")).then_inc(ctx_loaded, 16)
            sp.dma_start(wa[:], w_audio.rearrange("(k p) h -> p k h", p=P)).then_inc(wa_loaded, 16)
            for n, v in enumerate(VECS):
                sp.dma_start(vec_rows[n * KH:(n + 1) * KH, :], v.rearrange("(k p) -> k p", p=P)).then_inc(vec_loaded, 16)
            sp.dma_start(wo, w_out.rearrange("(k p) h -> p k h", p=P)).then_inc(wo_loaded, 16)

            def body(b, i, live):
                if live(0):
                    if isinstance(i, int) and i == 0:
                        if b == 0:
                            sp.wait_ge(wtT_psum, KH)
                            sp.wait_ge(lin_ready, KD)
                        if b == 2:
                            for k in range(KD):
                                at, n = OFFSET[k], D - k * P
                                for buf, made in ((proj_hi, g_hi), (proj_lo, g_lo)):
                                    sp.wait_ge(made, k + 1)
                                    one = f32(buf[:, 0:1, at:at + n])
                                    sp.dma_start(f32(buf[:, 1:B, at:at + n]), one.to_broadcast([P, B - 1, n])).then_inc(t_copied, 16)
                            sp.wait_ge(wo_ready, KH)
                    for t in range(T):
                        wait_if_positive(sp, hid_ready, T, i, T * (b - B) + t + 1)
                        src = x[b, bass.ds(i * ROWS, ROWS), :].rearrange("(p t) d -> p t d", t=T)[:, t, :]
                        sp.dma_start(xs[:, b, t, :], src).then_inc(x_loaded[b][t], 16)
                if isinstance(i, int) and (i, b) == (0, B - 1):
                    for n, (at, w) in enumerate(KEYS):
                        for made, src, dst in ((val_hi_ready, f32(vb_hi), val_hi), (val_lo_ready, vbuf, val_lo)):
                            sp.wait_ge(made, n + 1)
                            for q in range(B):
                                lo, hi = max(q * S, at), min((q + 1) * S, at + w)
                                if lo < hi:
                                    sp.dma_start(f32(dst[lo - q * S:hi - q * S, q, :]), src[lo - at:hi - at, n, :]).then_inc(val_placed, 16)
                if live(5) and not (isinstance(i, int) and B * i + b - 5 >= SHARED):
                    q, j = (b - 5) % B, i + (b - 5) // B
                    wait_if_positive(sp, out_ready, T, i, T * (b - 5) + T)
                    dst = out[q, bass.ds(j * ROWS, ROWS), :].rearrange("(p t) d -> p t d", t=T)
                    sp.dma_start(dst, zs[:, q, :, :]).then_inc(out_stored[q], 16)

            for b in range(B):
                body(b, 0, lambda lag, b=b: b - lag >= 0)
            for b in range(B):
                body(b, 1, lambda lag, b=b: B + b - lag >= 0)
            with sp.Fori(2, STEPS // B) as i:
                for b in range(B):
                    body(b, i, lambda lag: True)
            for k in range(2):
                for b in range(B):
                    body(b, STEPS // B + k, lambda lag, s=k * B + b: lag > 0 and s - lag < 0)
            for q, t, done, count in ((SHARED, 0, out_ready, T * SHARED + 1), (SHARED, 1, out_tail, 1),
                                      (SHARED + 1, 0, out_ready, T * SHARED + 2), (SHARED + 2, 0, out_tail, 2),
                                      (SHARED + 1, 1, out_tail, 3), (SHARED + 2, 1, out_tail, 4)):
                sp.wait_ge(done, count)
                dst = out[q % B, bass.ds(q // B * ROWS, ROWS), :].rearrange("(p t) d -> p t d", t=T)[:, t, :]
                sp.dma_start(dst, zs[:, q % B, t, :]).then_inc(out_stored[q % B], 16)
            for b in range(B):
                sp.wait_ge(out_stored[b], 16 * (PER_BATCH + (1 if b in (SHARED % B, (SHARED + 1) % B, (SHARED + 2) % B) else 0)))

        @block.gpsimd
        def _(pool):
            nc.gpsimd.memset(ident[:], 1.0).then_inc(pool_own, 1)
            nc.gpsimd.memset(mean_of, 1.0 / H).then_inc(ones_ready, 1)
            nc.gpsimd.memset(ones, 1.0).then_inc(ones_ready, 1)
            nc.gpsimd.memset(neg_half[:], -0.5).then_inc(pool_own, 1)
            pool.wait_ge(pool_own, 1)
            nc.gpsimd.affine_select(out=ident[:], in_=ident[:], compare_op=ALU.is_equal, fill=0.0, base=0,
                                    pattern=[[-1, P]], channel_multiplier=1).then_inc(ident_ready, 1)
            nc.gpsimd.memset(score_c[:, :, S:SW], 0.0).then_inc(extras_ready, 1)
            for buf in (proj_hi, proj_lo):
                for k in range(KD):
                    at = SCORE_AT[k]
                    nc.gpsimd.memset(f32(buf[:, :, at + S:at + SW]), 0.0).then_inc(pool_own, 1)
            pool.wait_ge(pool_own, 2 + 2 * KD)
            for k in range(KD):
                at = SCORE_AT[k] + NXBAR
                nc.gpsimd.memset(f32(proj_hi[:, :, at:at + 1]), -1.0 / D).then_inc(extras_ready, 1)
            for k in range(KH):
                pool.wait_ge(vT_ready, k + 1)
                pool.wait_ge(vT_hi_ready, k + 1)
                nc.gpsimd.tensor_tensor(vT_lo[:, k, :], vT[:, k, :], f32(vT_hi[:, k, :]), ALU.subtract).then_inc(vT_lo_ready, 1)
                pool.wait_ge(osums_ready, k + 1)
                nc.gpsimd.tensor_scalar(wo[:, k, :], wo[:, k, :], 1.0, osums[:, k:k + 1], ALU.mult, ALU.add).then_inc(wo_centred, 1)
            for k in range(KH):
                pool.wait_ge(wo_centred, k + 1)
                pool.wait_ge(wo_hi_ready, k + 1)
                nc.gpsimd.tensor_tensor(wo_lo[:, k, :], wo[:, k, :], f32(wo_hi[:, k, :]), ALU.subtract).then_inc(wo_ready, 1)
            pool.wait_ge(osums_ready, KH + 1)
            nc.gpsimd.tensor_scalar(bo_rows[:], bo_rows[:], 1.0, osums[:, KH:KH + 1], ALU.mult, ALU.add).then_inc(bo_ready, 1)
            pool.wait_ge(kvar_ready, 1)
            nc.gpsimd.tensor_tensor(krstd[:, 0:3], kvar[:, 0:3], neg_half[:, 0:3], ALU.pow).then_inc(krstd_ready, 1)
            pool.wait_ge(gs_loaded, 32)
            nc.gpsimd.tensor_scalar(gain[:], gain[:], float(H) ** 0.5, 0.0, ALU.mult, ALU.add).then_inc(gain_ready, 1)
            pool.wait_ge(gain_ready, 1)

            def add_shift(b, i, t):
                wait_if_positive(pool, zg_ready, T, i, T * (b - 4) + t + 1 - (1 if tail(i, b) and b == 2 else 0))
                nc.gpsimd.tensor_tensor(zs[:, (b - 4) % B, t, :], zs[:, (b - 4) % B, t, :], shift[:], ALU.add).then_inc(out_ready, 1)

            def body(b, i, live):
                if live(2):
                    q = (b - 2) % B
                    wait_if_positive(pool, var_ready, T, i, T * (b - 2) + T)
                    nc.gpsimd.tensor_tensor(rstd[:, q, :], var[:, q, :], neg_half[:, 0:T], ALU.pow).then_inc(rstd_ready, 1)
                if isinstance(i, int) and (i, b) == (STEPS // B, 1):
                    add_shift(0, i, T - 1)
                tiles = range(T) if not tail(i, b) else range(1) if b < B - 1 else ()
                for t in tiles if live(4) else ():
                    wait_if_positive(pool, z_ready, T, i, T * (b - 4) + t + 1)
                    nc.gpsimd.tensor_tensor(zs[:, (b - 4) % B, t, :], zs[:, (b - 4) % B, t, :], gain[:], ALU.mult).then_inc(zg_ready, 1)
                if live(4) and len(tiles) == T:
                    add_shift(b, i, 0)
                if live(3):
                    q = (b - 3) % B
                    wait_if_positive(pool, var2_ready, 1, i, b - 2)
                    nc.gpsimd.tensor_tensor(rstd2[:, q, :], var2[:, q, :], neg_half[:, 0:T], ALU.pow).then_inc(rstd2_ready, 1)
                    wait_if_positive(pool, rstd2_ready, 1, i, b - 2)
                    nc.gpsimd.tensor_tensor(shift2[:, q, :], sc[:, q, :, NXBAR], rstd2[:, q, :], ALU.mult).then_inc(shift2_ready, 1)
                if live(4) and tiles and not (isinstance(i, int) and (i, b) == (STEPS // B, 0)):
                    add_shift(b, i, len(tiles) - 1)

            pipeline(pool, body)

        @block.scalar
        def _(act):
            act.wait_ge(ones_ready, 1)
            nc.scalar.activation(waste_act[:, 0, 0:1], mean_of[:, 0:1], ACT.Exp).then_inc(act_own, 1)
            def load_row(row, v, loaded):
                act.dma_start(row[:], v.rearrange("(a h) -> a h", a=1).to_broadcast([P, H])).then_inc(loaded, 16)

            nc.scalar.activation(mean_r, mean_of, ACT.Copy).then_inc(mean_r_ready, 1)
            for n, k in enumerate((1, 3)):
                act.wait_ge(wt_loaded[k], 16)
                act.wait_ge(act_own, n + 1)
                nc.scalar.activation(waste_act[:, 0, :], wt[:, k, :], ACT.Copy, scale=-1.0 / H,
                                     accum_out=sums[:, k:k + 1]).then_inc(act_own, 1)
            for k in range(KA):
                act.wait_ge(cxT_psum, k + 1)
                nc.scalar.activation(cxT[:, k, :], V_BANK[k][:, 0:BS], ACT.Copy).then_inc(cxT_ready, 1)
            load_row(bt_rows, b_text, bt_loaded)
            load_row(bo_rows, b_out, bo_loaded)
            load_row(gain, g_out, gs_loaded)
            load_row(shift, beta_out, gs_loaded)
            for k in range(KH):
                act.wait_ge(wtT_psum, k + 1)
                nc.scalar.activation(wtT_hi[:, k, :], W_BANK[k], ACT.Copy).then_inc(wtT_hi_ready, 1)
            act.wait_ge(vec_ready, 1)
            act.wait_ge(act_own, 3)
            for k in range(KH + 1):
                if k < KH:
                    act.wait_ge(vT_psum, k + 1)
                    for dst, made in ((vT, vT_ready), (vT_hi, vT_hi_ready)):
                        nc.scalar.activation(dst[:, k, :], V_BANK[k][:, 0:BS], ACT.Identity,
                                             bias=vec_cols[:, 3 * KH + k:3 * KH + k + 1]).then_inc(made, 1)
                row = wo[:, k, :] if k < KH else bo_rows[:]
                act.wait_ge(wo_loaded if k < KH else bo_loaded, 16)
                if k >= 2:
                    act.wait_ge(osums_ready, k - 1)
                nc.scalar.activation(waste_act[:, k % 2, :], row, ACT.Copy, scale=-1.0 / H,
                                     accum_out=osums[:, k:k + 1]).then_inc(osums_ready, 1)

            def t_hi(k):
                act.wait_ge(g_psum, k + 1)
                for at, n, skip in T_PIECES[k]:
                    last = nc.scalar.activation(proj_hi[:, 0, at:at + n], W_BANK[k][:, skip:skip + n], ACT.Copy,
                                                scale=(1.0 if skip == 0 else 2.0) / H)
                last.then_inc(g_hi, 1)

            t_hi(0)
            for k in range(KH):
                act.wait_ge(kc_ready, k + 1)
                nc.scalar.activation(kSq[:, k, :], kT[:, k, :], ACT.Square).then_inc(ksq_ready, 1)
            for k in range(1, KD):
                t_hi(k)

            def value_hi(n):
                w = KEYS[n][1]
                act.wait_ge(val_ready, n + 1)
                nc.scalar.activation(vb_hi[0:w, n, :], vbuf[0:w, n, :], ACT.Copy).then_inc(val_hi_ready, 1)

            for k in range(KH):
                act.wait_ge(kn_ready, k + 1)
                nc.scalar.activation(kT[:, k, :], kT[:, k, :], ACT.Identity,
                                     bias=vec_cols[:, 2 * KH + k:2 * KH + k + 1]).then_inc(kT_ready, 1)
                if k >= 1:
                    act.wait_ge(kT_ready, k)
                    nc.scalar.activation(kg_hi[:, k - 1, :], kT[:, k - 1, :], ACT.Copy, scale=g1s[:, k - 1:k]).then_inc(kg_hi_ready, 1)
            act.wait_ge(kT_ready, KH)
            nc.scalar.activation(kg_hi[:, KH - 1, :], kT[:, KH - 1, :], ACT.Copy, scale=g1s[:, KH - 1:KH]).then_inc(kg_hi_ready, 1)
            for n in range(len(KEYS)):
                value_hi(n)
            act.wait_ge(cd_rows_psum, 1)
            nc.scalar.activation(cd_rows[:], C_BANK[0:2, 0:BS], ACT.Copy).then_inc(cd_rows_ready, 1)
            for k in range(KD):
                act.wait_ge(m_psum, k + 1)
                nc.scalar.activation(proj_hi[:, :, SCORE_AT[k]:SCORE_AT[k] + S],
                                     M_BANK[k][:, 0:BS].rearrange("p (b s) -> p b s", b=B), ACT.Copy).then_inc(m_hi, 1)

            def hi_part(b, i, t):
                wait_if_positive(act, xT_psum, T, i, T * b + t + 1)
                wait_if_positive(act, proj_psum, T, i, T * (b - 2) + t + 1)
                nc.scalar.activation(x_hi[:, b % 2, t, :], psT[:, t, :], ACT.Copy).then_inc(x_hi_ready, 1)

            def square(b, i, t):
                q = (b - 3) % B
                wait_if_positive(act, hid_ready, T, i, T * (b - 3) + t + 1)
                wait_if_positive(act, sq_ready, T, i, T * (b - 4) + t + 1)
                nc.scalar.activation(waste_act[:, t, :], hid[:, (b - 3) % 2, t, :], ACT.Square,
                                     bias=sc[:, q, t, NXBAR:NXBAR + 1],
                                     accum_out=sq_sum[:, q, t:t + 1]).then_inc(sq_ready, 1)

            def body(b, i, live):
                if live(0):
                    hi_part(b, i, 0)
                if live(3):
                    square(b, i, 0)
                if live(2):
                    q = (b - 2) % B
                    wait_if_positive(act, max_ready, 1, i, b - 1)
                    wait_if_positive(act, probT_psum, 1, i, b - 3)
                    for t in range(T):
                        nc.scalar.activation(prob[:, b % 2, t, :], logits[:, b % 2, t, :], ACT.Exp,
                                             bias=neg_max[:, q, t:t + 1],
                                             accum_out=prob_sum[:, q, t:t + 1]).then_inc(prob_ready, 1)
                if live(3):
                    square(b, i, 1)
                if live(2):
                    wait_if_positive(act, probT_psum, 1, i, b - 1)
                    wait_if_positive(act, mix_psum, T, i, T * (b - 4) + T)
                    nc.scalar.activation(prob_hi[:, b % 2, :], psE[0:S, 0:T * P], ACT.Copy).then_inc(prob_hi_ready, 1)
                if live(0):
                    hi_part(b, i, 1)
                if live(3):
                    q = (b - 3) % B
                    wait_if_positive(act, shift2_ready, 1, i, b - 2)
                    stored = i + (b - 3) // B
                    if not isinstance(stored, int) or stored > 0:
                        act.wait_ge(out_stored[q], 16 * stored)
                    for t in range(0 if tail(i, b) and b == 2 else T):
                        nc.scalar.activation(zs[:, q, t, :], hid[:, (b - 3) % 2, t, :], ACT.Identity,
                                             bias=shift2[:, q, t:t + 1], scale=rstd2[:, q, t:t + 1]).then_inc(z_ready, 1)

            for t in range(T):
                hi_part(0, 0, t)
            pipeline(act, body)

        @block.vector
        def _(dve):
            own = [0]

            def link(ins):
                own[0] += 1
                ins.then_inc(dve_own, 1)
                dve.wait_ge(dve_own, own[0])

            for n in range(2):
                k = 2 * n
                dve.wait_ge(wt_loaded[k], 16)
                link(nc.vector.reduce_sum(sums[:, 8 + k:9 + k], wt[:, k, :], axis=AX_X))
                link(nc.vector.tensor_scalar(sums[:, k:k + 1], sums[:, 8 + k:9 + k], -1.0 / H, None, ALU.mult))
                nc.vector.tensor_scalar(wt[:, k, :], wt[:, k, :], sums[:, k:k + 1], None, ALU.add).then_inc(wc_ready, 1)
                dve.wait_ge(act_own, n + 2)
                nc.vector.tensor_scalar(wt[:, k + 1, :], wt[:, k + 1, :], sums[:, k + 1:k + 2], None, ALU.add).then_inc(wc_ready, 1)
            dve.wait_ge(vec_psum, 1)
            nc.vector.tensor_copy(vec_cols[:], psE[:, 0:len(VECS) * KH]).then_inc(vec_ready, 1)
            dve.wait_ge(vec_ready, 1)
            nc.vector.tensor_scalar(g1s[:], vec_cols[:, 0:KH], SCALE, None, ALU.mult).then_inc(g1s_ready, 1)
            for k in range(KH):
                dve.wait_ge(wtT_hi_ready, k + 1)
                nc.vector.tensor_tensor(wtT_lo[:, k, :], W_BANK[k], f32(wtT_hi[:, k, :]), ALU.subtract).then_inc(wtT_lo_ready, 1)
            dve.wait_ge(bt_loaded, 16)
            link(nc.vector.reduce_sum(sums[:, 4:5], bt_rows[:], axis=AX_X))
            link(nc.vector.tensor_scalar(sums[:, 5:6], sums[:, 4:5], -1.0 / H, None, ALU.mult))
            nc.vector.tensor_scalar(bt_rows[:], bt_rows[:], sums[:, 5:6], None, ALU.add).then_inc(bc_ready, 1)
            dve.wait_ge(g1s_ready, 1)
            nc.vector.scalar_tensor_tensor(cd_cols[:, :, 0], vec_cols[:, 5 * KH:6 * KH], sums[:, 5:6], g1s[:], ALU.add, ALU.mult).then_inc(cd_cols_ready, 1)
            nc.vector.tensor_scalar(cd_cols[:, :, 1], vec_cols[:, 4 * KH:5 * KH], SCALE, None, ALU.mult).then_inc(cd_cols_ready, 1)
            for n in range(2):
                nc.vector.tensor_copy(pick[:, n, :], ident[0:2, n:n + 1].to_broadcast([2, P])).then_inc(pick_ready, 1)
            dve.wait_ge(bc_ready, 1)
            dve.wait_ge(wc_ready, KD)
            for k in range(KD):
                nc.vector.tensor_tensor_reduce(out=waste_dve[:, k, :], in0=wt[:, k, :], in1=bt_rows[:], scale=2.0 / H, scalar=0.0,
                                               op0=ALU.mult, op1=ALU.add, accum_out=lin[:, k:k + 1]).then_inc(lin_ready, 1)
            dve.wait_ge(lin_ready, KD)
            nc.vector.tensor_tensor_reduce(out=waste_dve[:, 0, :], in0=bt_rows[:], in1=bt_rows[:], scale=1.0 / H, scalar=EPS,
                                           op0=ALU.mult, op1=ALU.add, accum_out=sums[:, 6:7]).then_inc(dve_own, 1)
            own[0] += 1
            dve.wait_ge(extras_ready, 1 + KD)
            for k in range(KD):
                at = SCORE_AT[k] + LIN
                nc.vector.tensor_copy(proj_hi[:, :, at], lin[:, k:k + 1].to_broadcast([P, B])).then_inc(lin_hi_ready, 1)
            dve.wait_ge(dve_own, own[0])
            nc.vector.tensor_copy(score_c[:, :, LIN], sums[:, 6:7].to_broadcast([P, B]))
            dve.wait_ge(lin_hi_ready, KD)
            for k in range(KD):
                at = SCORE_AT[k] + LIN
                nc.vector.tensor_tensor(proj_lo[:, :, at], lin[:, k:k + 1].to_broadcast([P, B]),
                                        f32(proj_hi[:, :, at]), ALU.subtract).then_inc(lin_lo_ready, 1)

            for k in range(KH):
                dve.wait_ge(wo_centred, k + 1)
                nc.vector.tensor_copy(wo_hi[:, k, :], wo[:, k, :]).then_inc(wo_hi_ready, 1)

            def t_lo(k):
                dve.wait_ge(g_hi, k + 1)
                for at, n, skip in T_PIECES[k]:
                    last = nc.vector.scalar_tensor_tensor(proj_lo[:, 0, at:at + n], W_BANK[k][:, skip:skip + n],
                                                          (1.0 if skip == 0 else 2.0) / H, f32(proj_hi[:, 0, at:at + n]),
                                                          ALU.mult, ALU.subtract)
                last.then_inc(g_lo, 1)

            t_lo(0)
            dve.wait_ge(mean_psum, 1)
            for k in range(KH):
                nc.vector.tensor_tensor(kT[:, k, :], vT[:, k, :], psA[:, 0, 0:BS], ALU.subtract).then_inc(kc_ready, 1)
            for k in range(1, KH):
                dve.wait_ge(ksq_ready, k + 1)
                if k > 1:
                    dve.wait_ge(ksqsum_ready, k - 1)
                nc.vector.tensor_tensor(kSqSum, kSq[:, 0, :] if k == 1 else kSqSum, kSq[:, k, :], ALU.add).then_inc(ksqsum_ready, 1)
            link(nc.vector.memset(kvar[:], 1.0))
            t_lo(1)
            dve.wait_ge(kvar_psum, 1)
            for n, (at, w) in enumerate(KEYS):
                last = nc.vector.tensor_scalar(kvar[0:w, n:n + 1], psA[0:w, 1, n:n + 1], EPS, None, ALU.add)
            last.then_inc(kvar_ready, 1)
            for k in range(2, KD):
                t_lo(k)
            dve.wait_ge(krstd_ready, 1)
            for n, (at, w) in enumerate(KEYS):
                last = nc.vector.tensor_scalar(diag[0:w, at:at + w], ident[0:w, 0:w], krstd[0:w, n:n + 1], None, ALU.mult)
            last.then_inc(diag_ready, 1)
            dve.wait_ge(krows_psum, 1)
            for k in range(KH):
                nc.vector.scalar_tensor_tensor(kT[:, k, :], kT[:, k, :], vec_cols[:, KH + k:KH + k + 1], psA[:, 0, 0:BS],
                                               ALU.mult, ALU.mult).then_inc(kn_ready, 1)

            def value(n):
                w = KEYS[n][1]
                dve.wait_ge(val_psum, n + 1)
                nc.vector.tensor_tensor(vbuf[0:w, n, :], VAL_BANK[n][0:w, :], bo_rows[0:w, :], ALU.add).then_inc(val_ready, 1)

            def value_lo(n):
                w = KEYS[n][1]
                dve.wait_ge(val_hi_ready, n + 1)
                nc.vector.tensor_tensor(vbuf[0:w, n, :].bitcast(F32R), vbuf[0:w, n, :], f32(vb_hi[0:w, n, :]),
                                        ALU.subtract).then_inc(val_lo_ready, 1)

            dve.wait_ge(bo_ready, 1)
            value(0)
            for k in range(KH):
                dve.wait_ge(kg_hi_ready, k + 1)
                nc.vector.scalar_tensor_tensor(kg_lo[:, k, :], kT[:, k, :], g1s[:, k:k + 1], f32(kg_hi[:, k, :]),
                                               ALU.mult, ALU.subtract).then_inc(kg_lo_ready, 1)
            for n in range(1, len(KEYS)):
                value(n)
            for n in range(len(KEYS)):
                value_lo(n)
            for k in range(KD):
                dve.wait_ge(m_hi, k + 1)
                dst = slice(SCORE_AT[k], SCORE_AT[k] + S)
                nc.vector.tensor_tensor(proj_lo[:, :, dst], M_BANK[k][:, 0:BS].rearrange("p (b s) -> p b s", b=B),
                                        f32(proj_hi[:, :, dst]), ALU.subtract).then_inc(m_lo, 1)

            def lo_part(b, i, t):
                wait_if_positive(dve, x_hi_ready, T, i, T * b + t + 1)
                nc.vector.tensor_tensor(x_lo[:, b % 2, t, :], psT[:, t, :], f32(x_hi[:, b % 2, t, :]),
                                        ALU.subtract).then_inc(x_lo_ready, 1)

            def part_of_scores(b, i, t, lag):
                q = (b - lag) % B
                wait_if_positive(dve, projB_psum, T, i, T * (b - lag) + t + 1)
                nc.vector.tensor_tensor(sc_part[:, t, :], psB[:, YB:YB + SW], score_c[:, q, :], ALU.add).then_inc(part_ready, 1)

            def part_of_quad(b, i, t, lag):
                q = (b - lag) % B
                nc.vector.tensor_tensor_reduce(out=waste_dve[:, 2 * t + 1, 0:YB], in0=psB[:, 0:YB], in1=xs[:, q, t, 0:YB],
                                               scale=1.0, scalar=0.0, op0=ALU.mult, op1=ALU.add,
                                               accum_out=quad_b[:, q, t:t + 1]).then_inc(quadB_ready, 1)

            def bank_a(b, i, t, lag):
                q = (b - lag) % B
                wait_if_positive(dve, proj_psum, T, i, T * (b - lag) + t + 1)
                wait_if_positive(dve, part_ready, T, i, T * (b - lag) + t + 1)
                nc.vector.tensor_tensor(sc[:, q, t, :], psA[:, t, YW:YW + SW], sc_part[:, t, :], ALU.add).then_inc(sc_ready, 1)
                wait_if_positive(dve, quadB_ready, T, i, T * (b - lag) + t + 1)
                nc.vector.tensor_tensor_reduce(out=waste_dve[:, 2 * t, 0:YW], in0=psA[:, t, 0:YW], in1=xs[:, q, t, P:D],
                                               scale=1.0, scalar=quad_b[:, q, t:t + 1], op0=ALU.mult, op1=ALU.add,
                                               accum_out=quad_a[:, q, t:t + 1]).then_inc(quad_ready, 1)

            def variance(b, i, t, lag):
                q = (b - lag) % B
                wait_if_positive(dve, sc_ready, T, i, T * (b - lag) + t + 1)
                wait_if_positive(dve, quad_ready, T, i, T * (b - lag) + t + 1)
                nc.vector.tensor_scalar(var[:, q, t:t + 1], quad_a[:, q, t:t + 1], sc[:, q, t, LIN:LIN + 1], EPS,
                                        ALU.add, ALU.max).then_inc(var_ready, 1)

            def residual(b, i, t):
                q = (b - 3) % B
                wait_if_positive(dve, mix_psum, T, i, T * (b - 3) + t + 1)
                wait_if_positive(dve, inv_ready, 1, i, b - 2)
                nc.vector.scalar_tensor_tensor(hid[:, (b - 3) % 2, t, :], psO[:, t, :], inv_sum[:, q, t:t + 1],
                                               xs[:, q, t, :], ALU.mult, ALU.add).then_inc(hid_ready, 1)

            def body(b, i, live):
                if live(3):
                    residual(b, i, 0)
                if live(1):
                    part_of_scores(b, i, 0, 1)
                if live(2):
                    q = (b - 2) % B
                    wait_if_positive(dve, rstd_ready, 1, i, b - 1)
                    wait_if_positive(dve, prob_ready, T, i, T * (b - 4) + T)
                    for t in range(T):
                        nc.vector.scalar_tensor_tensor(logits[:, b % 2, t, :], sc[:, q, t, 0:S], rstd[:, q, t:t + 1],
                                                       score_d[:, q, :], ALU.mult, ALU.add).then_inc(logits_ready, 1)
                if live(1):
                    part_of_quad(b, i, 0, 1)
                if live(2):
                    wait_if_positive(dve, logits_ready, T, i, T * (b - 2) + T)
                    nc.vector.reduce_max(neg_max[:, q, :], logits[:, b % 2, :, :], axis=AX_X, negate=True).then_inc(max_ready, 1)
                if live(3):
                    residual(b, i, 1)
                if live(0):
                    lo_part(b, i, 0)
                if live(2):
                    wait_if_positive(dve, prob_ready, T, i, T * (b - 2) + T)
                    nc.vector.reciprocal(inv_sum[:, q, :], prob_sum[:, q, :]).then_inc(inv_ready, 1)
                if tail(i, b) and b == 1:
                    tail_gain(SHARED)
                if tail(i, b) and b == 2:
                    last_gain(0)
                if live(1):
                    bank_a(b, i, 0, 1)
                if live(3):
                    wait_if_positive(dve, sq_ready, T, i, T * (b - 3) + T)
                    nc.vector.tensor_scalar(var2[:, (b - 3) % B, :], sq_sum[:, (b - 3) % B, :], H * EPS, None, ALU.add).then_inc(var2_ready, 1)
                if live(2):
                    wait_if_positive(dve, prob_hi_ready, 1, i, b - 1)
                    nc.vector.tensor_tensor(prob_lo[:, b % 2, :], psE[0:S, 0:T * P], f32(prob_hi[:, b % 2, :]),
                                            ALU.subtract).then_inc(prob_lo_ready, 1)
                if tail(i, b) and b == 1:
                    tail_shift(SHARED, 1)
                if live(1):
                    variance(b, i, 0, 1)
                    part_of_scores(b, i, 1, 1)
                    part_of_quad(b, i, 1, 1)
                    bank_a(b, i, 1, 1)
                if live(0):
                    lo_part(b, i, 1)
                if live(1):
                    variance(b, i, 1, 1)

            LAST = STEPS - 1

            def tail_gain(q):
                dve.wait_ge(z_ready, T * q + T)
                nc.vector.tensor_tensor(zs[:, q % B, 1, :], zs[:, q % B, 1, :], gain[:], ALU.mult).then_inc(zg_tail, 1)

            def tail_shift(q, gains):
                dve.wait_ge(zg_tail, gains)
                nc.vector.tensor_tensor(zs[:, q % B, 1, :], zs[:, q % B, 1, :], shift[:], ALU.add).then_inc(out_tail, 1)

            def last_gain(t):
                dve.wait_ge(out_stored[LAST % B], 16 * (PER_BATCH - 1))
                dve.wait_ge(hid_ready, T * LAST + t + 1)
                nc.vector.scalar_tensor_tensor(zs[:, LAST % B, t, :], hid[:, LAST % 2, t, :], sc[:, LAST % B, t, NXBAR:NXBAR + 1],
                                               gain[:], ALU.add, ALU.mult).then_inc(zg_tail, 1)

            def last_scale(t):
                nc.vector.scalar_tensor_tensor(zs[:, LAST % B, t, :], zs[:, LAST % B, t, :], rstd2[:, LAST % B, t:t + 1], shift[:],
                                               ALU.mult, ALU.add).then_inc(out_tail, 1)

            def finish():
                last_gain(1)
                tail_gain(SHARED + 1)
                dve.wait_ge(zg_tail, 3)
                dve.wait_ge(rstd2_ready, STEPS)
                last_scale(0)
                tail_shift(SHARED + 1, 4)
                last_scale(1)

            for t in range(T):
                lo_part(0, 0, t)
            dve.wait_ge(cd_psum, 1)
            nc.vector.tensor_copy(score_c[:, :, 0:S], C_BANK[:, 0:BS].rearrange("p (b s) -> p b s", b=B)).then_inc(cd_ready, 1)
            dve.wait_ge(cd_psum, 2)
            nc.vector.tensor_copy(score_d[:], D_BANK[:, 0:BS].rearrange("p (b s) -> p b s", b=B)).then_inc(cd_ready, 1)
            dve.wait_ge(cd_ready, 2)
            pipeline(dve, body)
            finish()

        @block.tensor
        def _(pe):
            def parts3(a_hi, a_lo, b_hi, b_lo):
                return (a_hi, b_hi), (a_hi, b_lo), (a_lo, b_hi)

            def keep_busy(count):
                for n in range(count):
                    nc.tensor.matmul(psB[:, 0:P], ident[:], ident[:], start=True, stop=True)

            pe.wait_ge(ident_ready, 1)
            keep_busy(8)
            for j in range(KD):
                if j == 2:
                    pe.wait_ge(ctx_loaded, 16)
                    for k in range(KA):
                        for b in range(B):
                            last = nc.tensor.transpose(V_BANK[k][:, b * S:(b + 1) * S], cx[:, b, k * P:(k + 1) * P], ident[0:S, 0:S])
                        last.then_inc(cxT_psum, 1)
                pe.wait_ge(wc_ready, j + 1)
                for k in range(KH):
                    last = nc.tensor.transpose(W_BANK[k][:, j * P:(j + 1) * P], wt[:, j, k * P:(k + 1) * P], ident[:])
                    if j == KD - 1:
                        last.then_inc(wtT_psum, 1)
            pe.wait_ge(vec_loaded, 16 * len(VECS))
            nc.tensor.transpose(psE[:, 0:len(VECS) * KH], vec_rows[:], ident[0:len(VECS) * KH, 0:len(VECS) * KH]).then_inc(vec_psum, 1)
            pe.wait_ge(wa_loaded, 16)
            pe.wait_ge(cxT_ready, KA)
            for k in range(KH):
                if k == KH - 1:
                    pe.wait_ge(vec_ready, 1)
                for j in range(KA):
                    last = nc.tensor.matmul(V_BANK[k][:, 0:BS], wa[:, j, k * P:(k + 1) * P], cxT[:, j, :],
                                            start=(j == 0), stop=(j == KA - 1))
                last.then_inc(vT_psum, 1)

            def gram(k):
                passes = [(h, a, w) for h in range(KH) for a, w in parts3(wtT_hi, wtT_lo, wtT_hi, wtT_lo)]
                for n, (h, a, w) in enumerate(passes):
                    last = nc.tensor.matmul(W_BANK[k][:, 0:D - k * P], a[:, h, k * P:(k + 1) * P], w[:, h, k * P:D],
                                            start=(n == 0), stop=(n == len(passes) - 1))
                last.then_inc(g_psum, 1)

            pe.wait_ge(wtT_lo_ready, KH)
            gram(0)
            pe.wait_ge(mean_r_ready, 1)
            pe.wait_ge(vT_hi_ready, KH)
            pe.wait_ge(vT_lo_ready, KH)
            passes = [(k, v) for v in (vT_hi, vT_lo) for k in range(KH)]
            for n, (k, v) in enumerate(passes):
                last = nc.tensor.matmul(psA[:, 0, 0:BS], mean_r, v[:, k, :], start=(n == 0), stop=(n == len(passes) - 1))
            last.then_inc(mean_psum, 1)
            pe.wait_ge(ones_ready, 2)
            for k in range(1, KD):
                gram(k)
            pe.wait_ge(ksqsum_ready, KH - 1)
            for n, (at, w) in enumerate(KEYS):
                last = nc.tensor.matmul(psA[0:w, 1, n:n + 1], kSqSum[:, at:at + w], mean_of[:, 0:1], start=True, stop=True)
            last.then_inc(kvar_psum, 1)
            def values_product(n):
                at, keys = KEYS[n]
                passes = [(h, a, w) for h in range(KH) for a, w in parts3(vT_hi, vT_lo, wo_hi, wo_lo)]
                for m, (h, a, w) in enumerate(passes):
                    last = nc.tensor.matmul(VAL_BANK[n][0:keys, :], a[:, h, at:at + keys], w[:, h, :],
                                            start=(m == 0), stop=(m == len(passes) - 1))
                last.then_inc(val_psum, 1)

            pe.wait_ge(wo_ready, KH)
            pe.wait_ge(g_lo, 2)
            values_product(0)
            pe.wait_ge(diag_ready, 1)
            for at, w in KEYS:
                last = nc.tensor.matmul(psA[:, 0, at:at + w], ones[0:w, :], diag[0:w, at:at + w], start=True, stop=True)
            last.then_inc(krows_psum, 1)
            values_product(1)
            pe.wait_ge(kvar_ready, 1)
            values_product(2)
            pe.wait_ge(cd_cols_ready, 2)
            pe.wait_ge(kT_ready, KH)
            for h in range(KH):
                last = nc.tensor.matmul(C_BANK[0:2, 0:BS], cd_cols[:, h, :], kT[:, h, :], start=(h == 0), stop=(h == KH - 1))
            last.then_inc(cd_rows_psum, 1)
            pe.wait_ge(kg_lo_ready, KH)
            pe.wait_ge(g_lo, KD)
            passes = [(h, a, w) for h in range(KH) for a, w in parts3(wtT_hi, wtT_lo, kg_hi, kg_lo)]
            for k in range(KD):
                if k == KD - 1:
                    pe.wait_ge(val_ready, len(KEYS))
                for n, (h, a, w) in enumerate(passes):
                    last = nc.tensor.matmul(M_BANK[k][:, 0:BS], a[:, h, k * P:(k + 1) * P], w[:, h, :],
                                            start=(n == 0), stop=(n == len(passes) - 1))
                last.then_inc(m_psum, 1)

            def transpose_x(b, i, t):
                pe.wait_ge(x_loaded[b][t], 16 * (i + 1))
                wait_if_positive(pe, x_lo_ready, T, i, T * (b - 1) + t + 1)
                for k in range(KD):
                    last = nc.tensor.transpose(psT[:, t, k * P:(k + 1) * P], xs[:, b, t, k * P:(k + 1) * P], ident[:])
                last.then_inc(xT_psum, 1)

            for t in range(T):
                transpose_x(0, 0, t)
            pe.wait_ge(pick_ready, 2)
            pe.wait_ge(cd_rows_ready, 1)
            nc.tensor.matmul(C_BANK[:, 0:BS], pick[:, 0, :], cd_rows[:], start=True, stop=True).then_inc(cd_psum, 1)
            pe.wait_ge(m_lo, 1)
            nc.tensor.matmul(D_BANK[:, 0:BS], pick[:, 1, :], cd_rows[:], start=True, stop=True).then_inc(cd_psum, 1)
            pe.wait_ge(m_lo, KD)
            pe.wait_ge(lin_lo_ready, KD)

            PASSES = [(a, w, k) for k in (1, 0, 2, 3) for a, w in parts3(x_hi, x_lo, proj_hi, proj_lo)]

            def project_b(b, i, t):
                q, par = (b - 1) % B, (b - 1) % 2
                if isinstance(i, int) and (i, b, t) == (0, 2, 0):
                    pe.wait_ge(t_copied, 2 * 16 * KD)
                wait_if_positive(pe, x_lo_ready, T, i, T * (b - 1) + t + 1)
                wait_if_positive(pe, quadB_ready, T, i, T * (b - 1) + t)
                for n, (part, w) in enumerate(parts3(x_hi, x_lo, proj_hi, proj_lo)):
                    last = nc.tensor.matmul(psB[:, 0:YB + SW], part[:, par, t, 0:P], w[:, q, BANK_B:BANK_B + YB + SW],
                                            start=(n == 0), stop=(n == 2))
                last.then_inc(projB_psum, 1)

            def project_a(b, i, t):
                q, par = (b - 1) % B, (b - 1) % 2
                wait_if_positive(pe, quad_ready, T, i, T * (b - 2) + t + 1)
                for n, (part, w, k) in enumerate(PASSES):
                    last = nc.tensor.matmul(psA[:, t, SKIP[k]:SKIP[k] + WIDTH[k]], part[:, par, t, k * P:(k + 1) * P],
                                            w[:, q, OFFSET[k]:OFFSET[k] + WIDTH[k]], start=(n == 0), stop=(n == len(PASSES) - 1))
                last.then_inc(proj_psum, 1)

            def body(b, i, live):
                if live(0):
                    transpose_x(b, i, 0)
                if live(1):
                    project_b(b, i, 0)
                    project_a(b, i, 0)
                if live(0):
                    transpose_x(b, i, 1)
                if live(1):
                    project_b(b, i, 1)
                if tail(i, b) and b == 1:
                    pe.wait_ge(quadB_ready, T * STEPS)
                    keep_busy(9)
                if live(2):
                    wait_if_positive(pe, prob_ready, T, i, T * (b - 2) + T)
                    wait_if_positive(pe, prob_lo_ready, 1, i, b - 2)
                    for t in range(T):
                        last = nc.tensor.transpose(psE[0:S, t * P:(t + 1) * P], prob[:, b % 2, t, :], ident[:])
                    last.then_inc(probT_psum, 1)
                if live(1):
                    project_a(b, i, 1)
                if tail(i, b) and b == 1:
                    keep_busy(5)
                if live(2):
                    q = (b - 2) % B
                    wait_if_positive(pe, prob_lo_ready, 1, i, b - 1)
                    if isinstance(i, int) and (i, b) == (0, 2):
                        pe.wait_ge(val_placed, 2 * 16 * SEGMENTS)
                    for t in range(T):
                        wait_if_positive(pe, hid_ready, T, i, T * (b - 3) + t + 1)
                        for n, (pr, v) in enumerate(((prob_hi, val_hi), (prob_hi, val_lo), (prob_lo, val_hi))):
                            last = nc.tensor.matmul(psO[:, t, :], pr[:, b % 2, t * P:(t + 1) * P], v[:, q, :],
                                                    start=(n == 0), stop=(n == 2))
                        last.then_inc(mix_psum, 1)

            pipeline(pe, body)


_PRE = "L0_xattn_"
_INS = ["x", "ctx_768"] + [_PRE + n for n in ("W_text", "b_text", "W_audio", "b_audio", "W_out", "b_out",
                                              "g1", "beta1", "g2", "beta2", "g_out", "beta_out")]


def kernel(**inputs):
    import numpy as _np
    import concourse.bacc as _bacc
    from concourse import mybir as _mybir
    from concourse.bass_utils import run_bass_kernel_spmd as _run

    nc = _bacc.Bacc("TRN2", target_bir_lowering=False, num_devices=1)
    arrays, args = {}, []
    for name in _INS:
        a = _np.ascontiguousarray(inputs[name])
        arrays[f"in_{name}_dram"] = a
        args.append(nc.dram_tensor(f"in_{name}_dram", a.shape, _mybir.dt.from_np(a.dtype), kind="ExternalInput").ap())
    shape = inputs["x"].shape
    args.append(nc.dram_tensor("out_dram", shape, _mybir.dt.float32, kind="ExternalOutput").ap())
    cross_attention(nc, *args)
    r = _run(nc, [arrays], core_ids=[0])
    return r.results[0]["out_dram"]
```
